# Optimizing a Trainium2 kernel written in Bass

```python
import numpy as np
import jax
import jax.numpy as jnp

def _softmax(x, axis=-1):
    return jax.nn.softmax(x, axis=axis)

def _gelu(x):
    return jax.nn.gelu(x, approximate=True)

def _silu(x):
    return jax.nn.silu(x)

def _sigmoid(x):
    return jax.nn.sigmoid(x)

def _layernorm(x, axis=-1, eps=1e-05):
    m = jnp.mean(x, axis=axis, keepdims=True)
    v = jnp.var(x, axis=axis, keepdims=True)
    return (x - m) / jnp.sqrt(v + eps)

def _scatter_add(tgt, idx, src, axis=0):
    return tgt.at[idx].add(src)

def _segment_sum(src, seg, n):
    return jax.ops.segment_sum(src, seg, n)
kernel_name = 'mk_adj_resnorm_d2_adj_r2_97401a'

def setup_inputs(seed: int=0):
    np.random.seed(seed)
    _w = jnp.asarray

    def _rec_inputs():
        import jax
        import jax.numpy as jnp
        _gk = jax.random.key(seed)
        x = -0.0001538 + 1 * jax.random.normal(jax.random.fold_in(_gk, 1), (8, 1024, 384), jnp.float32)
        _a = jax.random.bernoulli(jax.random.fold_in(_gk, 2), 0.00390625, (8, 1024, 1024))
        _a = jnp.logical_or(_a, jnp.swapaxes(_a, -1, -2))
        _a = jnp.logical_or(_a, jnp.eye(1024, dtype=bool))
        _af = _a.astype(jnp.float32)
        _af = _af * jax.random.uniform(jax.random.fold_in(_gk, 3), (8, 1024, 1024), jnp.float32, 0.05, 4.42607)
        adj = _af
        return (x, adj)
    x, adj = _rec_inputs()

    def _L0_gnn_setup():
        import jax, jax.numpy as jnp
        import numpy as np
        NUM_HEADS = 12
        HIDDEN = 384
        HEAD = HIDDEN // NUM_HEADS
        B, N = (16, 256)
        key = jax.random.key(seed)
        ks = jax.random.split(key, 9)
        s = 0.02
        return {'x': jax.random.normal(ks[0], (B, N, HIDDEN), jnp.float32), 'spatial_encoding': jax.random.normal(ks[1], (B, N, N), jnp.float32), 'edge_encoding': jax.random.normal(ks[2], (B, N, N), jnp.float32), 'Wq': jax.random.normal(ks[3], (HIDDEN, HIDDEN), jnp.float32) * s, 'Wk': jax.random.normal(ks[4], (HIDDEN, HIDDEN), jnp.float32) * s, 'Wv': jax.random.normal(ks[5], (HIDDEN, HIDDEN), jnp.float32) * s, 'bv': jax.random.normal(ks[6], (HIDDEN,), jnp.float32) * s, 'Wo': jax.random.normal(ks[7], (HIDDEN, HIDDEN), jnp.float32) * s, 'bo': jax.random.normal(ks[8], (HIDDEN,), jnp.float32) * s}
    _L0_gnn_all = _L0_gnn_setup()
    _L0_gnn_in = {k: v for k, v in _L0_gnn_all.items() if k in ('Wq', 'Wk', 'Wv', 'bv', 'Wo', 'bo')}
    del _L0_gnn_all

    def _L1_gnn_setup():
        import jax, jax.numpy as jnp
        import numpy as np
        NUM_HEADS = 12
        HIDDEN = 384
        HEAD = HIDDEN // NUM_HEADS
        SCALE = HIDDEN ** (-0.5)
        key = jax.random.key(seed)
        ks = jax.random.split(key, 8)
        B, N = (16, 256)
        std = HIDDEN ** (-0.5)
        return {'x': jax.random.normal(ks[0], (B, N, HIDDEN), dtype=jnp.float32), 'encoding_bias': jax.random.normal(ks[1], (B, N, N), dtype=jnp.float32), 'Wq': jax.random.normal(ks[2], (HIDDEN, HIDDEN), dtype=jnp.float32) * std, 'Wk': jax.random.normal(ks[3], (HIDDEN, HIDDEN), dtype=jnp.float32) * std, 'Wv': jax.random.normal(ks[4], (HIDDEN, HIDDEN), dtype=jnp.float32) * std, 'bv': jax.random.normal(ks[5], (HIDDEN,), dtype=jnp.float32) * 0.01, 'Wo': jax.random.normal(ks[6], (HIDDEN, HIDDEN), dtype=jnp.float32) * std, 'bo': jax.random.normal(ks[7], (HIDDEN,), dtype=jnp.float32) * 0.01}
    _L1_gnn_all = _L1_gnn_setup()
    _L1_gnn_in = {k: v for k, v in _L1_gnn_all.items() if k in ('Wq', 'Wk', 'Wv', 'bv', 'Wo', 'bo')}
    del _L1_gnn_all
    return {'x': x, 'adj': adj, 'L0_gnn_Wq': _L0_gnn_in['Wq'], 'L0_gnn_Wk': _L0_gnn_in['Wk'], 'L0_gnn_Wv': _L0_gnn_in['Wv'], 'L0_gnn_bv': _L0_gnn_in['bv'], 'L0_gnn_Wo': _L0_gnn_in['Wo'], 'L0_gnn_bo': _L0_gnn_in['bo'], 'L1_gnn_Wq': _L1_gnn_in['Wq'], 'L1_gnn_Wk': _L1_gnn_in['Wk'], 'L1_gnn_Wv': _L1_gnn_in['Wv'], 'L1_gnn_bv': _L1_gnn_in['bv'], 'L1_gnn_Wo': _L1_gnn_in['Wo'], 'L1_gnn_bo': _L1_gnn_in['bo']}

def reference(x, adj, L0_gnn_Wq, L0_gnn_Wk, L0_gnn_Wv, L0_gnn_bv, L0_gnn_Wo, L0_gnn_bo, L1_gnn_Wq, L1_gnn_Wk, L1_gnn_Wv, L1_gnn_bv, L1_gnn_Wo, L1_gnn_bo):
    import jax
    import jax.numpy as jnp

    def _L0_gnn_ref(x, spatial_encoding, edge_encoding, Wq, Wk, Wv, bv, Wo, bo):
        import jax, jax.numpy as jnp
        import numpy as np
        NUM_HEADS = 12
        HIDDEN = 384
        HEAD = HIDDEN // NUM_HEADS
        B, N = (16, 256)
        b, n, h = x.shape
        scale = jnp.asarray(HIDDEN, x.dtype) ** (-0.5)
        q = (x @ Wq.T).reshape(b, n, NUM_HEADS, HEAD)
        k = (x @ Wk.T).reshape(b, n, NUM_HEADS, HEAD)
        v = (x @ Wv.T + bv).reshape(b, n, NUM_HEADS, HEAD)
        bias = (spatial_encoding + edge_encoding)[:, None]
        scores = jnp.einsum('bqhd,bkhd->bhqk', q, k) * scale + bias
        row_nonzero = jnp.any(scores != 0, axis=-1, keepdims=True)
        scores = jnp.where(row_nonzero, scores, -jnp.inf)
        p = jax.nn.softmax(scores, axis=-1)
        p = jnp.nan_to_num(p)
        out = jnp.einsum('bhqk,bkhd->bqhd', p, v).reshape(b, n, h)
        return out @ Wo.T + bo

    def _L1_gnn_ref(x, encoding_bias, Wq, Wk, Wv, bv, Wo, bo):
        import jax, jax.numpy as jnp
        import numpy as np
        NUM_HEADS = 12
        HIDDEN = 384
        HEAD = HIDDEN // NUM_HEADS
        SCALE = HIDDEN ** (-0.5)
        B, N, _ = x.shape
        q = (x @ Wq.T).reshape(B, N, NUM_HEADS, HEAD)
        k = (x @ Wk.T).reshape(B, N, NUM_HEADS, HEAD)
        v = (x @ Wv.T + bv).reshape(B, N, NUM_HEADS, HEAD)
        a = jnp.einsum('bnhd,bmhd->bhnm', q, k) * SCALE + encoding_bias[:, None, :, :]
        pad_mask = jnp.all(a == 0, axis=-1)
        a = jnp.where(pad_mask[..., None], -jnp.inf, a)
        a = jax.nn.softmax(a, axis=-1)
        a = jnp.nan_to_num(a)
        o = jnp.einsum('bhnm,bmhd->bnhd', a, v).reshape(B, N, HIDDEN)
        return o @ Wo.T + bo
    x = _layernorm(x + _L0_gnn_ref(x, adj, adj, L0_gnn_Wq, L0_gnn_Wk, L0_gnn_Wv, L0_gnn_bv, L0_gnn_Wo, L0_gnn_bo), axis=-1)
    x = _layernorm(x + _L1_gnn_ref(x, adj, L1_gnn_Wq, L1_gnn_Wk, L1_gnn_Wv, L1_gnn_bv, L1_gnn_Wo, L1_gnn_bo), axis=-1)
    return x

_drawn_inputs = setup_inputs


def setup_inputs(seed=0):
    import zlib

    import numpy as np

    out = dict(_drawn_inputs(seed))
    spreads = {}
    factors = {'L0_gnn_Wq': 8.0,
     'L0_gnn_Wk': 8.0,
     'L0_gnn_bv': 4.729,
     'L1_gnn_bv': 5.127,
     'L1_gnn_bo': 5.658}
    for name, (base, spread) in spreads.items():
        noise = np.random.default_rng([zlib.crc32(name.encode()), seed]).standard_normal(out[name].shape)
        drawn = base * np.exp(spread * noise) if base else spread * noise
        out[name] = jnp.asarray(drawn.astype(out[name].dtype))
    for name, factor in factors.items():
        out[name] = (out[name] * factor).astype(out[name].dtype)
    return out
```

```python
from contextlib import ExitStack

import concourse.bass as bass
from concourse import mybir

P = 128
LAYERS, BATCH, TOKENS, HIDDEN, HEADS = 2, 8, 1024, 384, 12
HEAD = HIDDEN // HEADS
STEPS = LAYERS * BATCH
KT = HIDDEN // P
TILES = TOKENS // P
GROUP = P // HEAD
GROUPS = HEADS // GROUP
HALF = TOKENS // 2
CHUNK = 2 * GROUP
CHUNKS = GROUPS * TILES // 2
CHUNKS_OF_GROUP = CHUNKS // GROUPS
ITEMS = CHUNKS * CHUNK
ITEMS_OF_GROUP = ITEMS // GROUPS
PAIR_Q = 2 * P
RING = 3
EPS = 1e-5
SCALE = float(HIDDEN) ** -0.5

F32 = mybir.dt.float32
F32R = mybir.dt.float32r
ACT = mybir.ActivationFunctionType
ALU = mybir.AluOpType

SLOT_Q1 = 3
SLOT_K0, SLOT_K1, SLOT_Q0 = 13, 17, 21
SLOT_X = 68
SLOT_V = 2
SLOT_O = [77, 78, 85, 86, 93, 94, ITEMS + 5, ITEMS + 6]


def turns_of_frame():
    turns = [(SLOT_V + t, 2, "V", t, 0) for t in range(TILES)]
    turns += [(SLOT_X + t, 2, "X", t, 1) for t in range(TILES)]
    for g in range(GROUPS):
        turns.append((ITEMS_OF_GROUP * g + SLOT_Q1, 1, "P", 4 * g + 3, 0))
        for j, slot in enumerate((SLOT_K0, SLOT_K1, SLOT_Q0)):
            nxt = (g + 1) % GROUPS
            turns.append((ITEMS_OF_GROUP * g + slot, 2, "P", 4 * nxt + j, 0 if nxt else 1))
    for c in range(CHUNKS):
        slot = CHUNK * c + CHUNK + 2
        turns.append((slot % ITEMS, 1, "R", c, -(slot // ITEMS)))
    for t, slot in enumerate(SLOT_O):
        turns.append((slot % ITEMS, 1, "O", t, -(slot // ITEMS)))
    return sorted(turns)


TURNS = turns_of_frame()
BEFORE = sum(1 for t in TURNS if t[4] == 1) - sum(1 for t in TURNS if t[4] == -1)


class Frame:

    def __init__(self, pair, odd, first=0, last=0):
        self.pair, self.odd = pair, odd
        self.f = 2 * pair + odd if isinstance(pair, int) else None
        f = self.f
        self.prev = f is None or f > 0
        self.cur = f is None or 0 <= f < STEPS
        self.next = f is None or f < STEPS - 1
        self.slots = ITEMS if f is None or f < STEPS else 10

    def count(self, per_step, n):
        return self.pair * (2 * per_step) + (self.odd * per_step + n)

    def has(self, off):
        return (self.prev, self.cur, self.next)[off + 1]

    def turn(self, kind, index, off=0):
        at = next(n for n, t in enumerate(TURNS) if t[2] == kind and t[3] == index)
        frame_off = off - TURNS[at][4]
        if self.f is None:
            return self.count(len(TURNS), frame_off * len(TURNS) + BEFORE + at + 1)
        return sum(1 for f in range(-1, self.f + frame_off + 1)
                   for t in (TURNS if f < self.f + frame_off else TURNS[:at + 1]) if 0 <= f + t[4] < STEPS)

    def turns_at(self, slot, window):
        return [(k, i, off) for s, w, k, i, off in TURNS if s == slot and w == window and self.has(off)]


def wait(eng, sem, value):
    if not (isinstance(value, int) and value <= 0):
        eng.wait_ge(sem, value)


def settle(eng, fr, counter):
    if fr.f is None:
        eng.sem_inc(counter, 1)


def run_frames(eng, frame_program):
    frame_program(Frame(-1, 1))
    frame_program(Frame(0, 0))
    frame_program(Frame(0, 1))
    with eng.Fori(1, STEPS // 2 - 1) as pair:
        frame_program(Frame(pair, 0))
        frame_program(Frame(pair, 1))
    frame_program(Frame(STEPS // 2 - 1, 0))
    frame_program(Frame(STEPS // 2 - 1, 1))
    frame_program(Frame(STEPS // 2, 0))


def item_of(n):
    chunk = n // CHUNK
    return chunk // CHUNKS_OF_GROUP, (n % CHUNK) // 2, 2 * (chunk % CHUNKS_OF_GROUP) + n % 2


def before(n, lag):
    return (n - lag, 0) if n >= lag else (n - lag + ITEMS, -1)


def build(nc, x, adj, weights, biases, layer_consts, identity, out):
    ctx = ExitStack()
    with ctx:
        def sb(name, shape, dt=F32):
            return ctx.enter_context(nc.sbuf_tensor(name, shape, dt))

        def psum(name, shape):
            return ctx.enter_context(nc.psum_tensor(name, shape, F32))

        def sem(name):
            return ctx.enter_context(nc.semaphore(name))

        ident = sb("ident", [P, P])
        x_in = sb("x_in", [P, 2, HIDDEN])
        x_turned = sb("x_turned", [P, KT, TOKENS])
        w_qk = sb("w_qk", [P, 2, KT, HIDDEN])
        w_v = sb("w_v", [P, KT, HIDDEN])
        w_o = sb("w_o", [P, KT, HIDDEN])
        bias_v = sb("bias_v", [P, HIDDEN])
        bias_o = sb("bias_o", [P, HIDDEN])
        consts = sb("consts", [P, 2, 2])
        part_hi = sb("part_hi", [P, 2, HALF], F32R)
        part_lo = sb("part_lo", [P, 2, HALF], F32R)
        k_stack = sb("k_stack", [P, 2, GROUP, TOKENS], F32R)
        q_stack = sb("q_stack", [P, 2, GROUP, HALF], F32R)
        adj_sb = sb("adj_sb", [P, TILES, TOKENS])
        probs = sb("probs", [P, RING, TOKENS])
        neg_max = sb("neg_max", [P, 2, CHUNK])
        row_sum = sb("row_sum", [P, 2, CHUNK])
        inverse = sb("inverse", [P, 2, CHUNK])
        guard = sb("guard", [P, 3, CHUNK])
        inverse_wide = sb("inverse_wide", [P, 2, GROUP, HEAD])
        inverse_turned = sb("inverse_turned", [P, PAIR_Q])
        probs_turned = sb("probs_turned", [P, CHUNK, TILES, P])
        values = sb("values", [P, TILES, HIDDEN])
        out_turned = sb("out_turned", [P, GROUPS, TOKENS])
        res = sb("res", [P, 2, HIDDEN])
        stats = sb("stats", [P, 2, 6])
        mean_var = sb("mean_var", [P, 2, 2])
        rstd = sb("rstd", [P, 2, 2])
        minus_half = sb("minus_half", [P, 1])

        ps_scores = psum("ps_scores", [P, 2, TOKENS])
        ps_turn = psum("ps_turn", [P, 2, HALF])
        ps_out = psum("ps_out", [P, HALF])
        ps_shared = psum("ps_shared", [P, HALF])

        ident_loaded = sem("ident_loaded")
        x_loaded = [sem(f"x_loaded{i}") for i in range(2)]
        wqk_loaded = sem("wqk_loaded")
        wv_loaded = sem("wv_loaded")
        wo_loaded = sem("wo_loaded")
        consts_loaded = sem("consts_loaded")
        stacked = [sem(f"stacked_{n}") for n in ("k0", "k1", "q0", "q1")]
        adj_loaded = [sem(f"adj_loaded{j}") for j in range(TILES // 2)]
        res_loaded = [sem(f"res_loaded{i}") for i in range(2)]
        shared_filled = sem("shared_filled")
        shared_drained = sem("shared_drained")
        hi_ready = sem("hi_ready")
        scores_ready = sem("scores_ready")
        shifted_ready = sem("shifted_ready")
        probs_ready = sem("probs_ready")
        turned_a = sem("turned_a")
        turned_b = sem("turned_b")
        moved_a = sem("moved_a")
        moved_b = sem("moved_b")
        pv_ready = sem("pv_ready")
        out_moved = sem("out_moved")
        inverse_ready = sem("inverse_ready")
        guard_step = sem("guard_step")
        wide_ready = sem("wide_ready")
        res_ready = sem("res_ready")
        stats_step = sem("stats_step")
        stats_ready = sem("stats_ready")
        norm_step = sem("norm_step")
        half_set = sem("half_set")
        out_stored = [sem(f"out_stored{i}") for i in range(2)]

        sp_settled, dve_settled, pool_settled = sem("sp_settled"), sem("dve_settled"), sem("pool_settled")

        block = ctx.enter_context(nc.Block())

        @block.sync
        def _(sp):
            def sp_wait(fr, sem, value):
                wait(sp, sem, value)
                settle(sp, fr, sp_settled)

            def stack_dmas(fr, index, off):
                g, j = divmod(index, 4)
                buf = j % 2
                group = fr.count(GROUPS, GROUPS * off + g)
                sp_wait(fr, shared_drained, fr.turn("P", index, off))
                done = fr.count(ITEMS, ITEMS * off + ITEMS_OF_GROUP * g)
                sp_wait(fr, scores_ready, done - (ITEMS_OF_GROUP, ITEMS_OF_GROUP, ITEMS_OF_GROUP // 2, 0)[j])
                for block_row in range(4):
                    low = block_row % 2 if j >= 2 else block_row // 2
                    part = part_lo if low else part_hi
                    rows = slice(HEAD * block_row, HEAD * (block_row + 1))
                    for h in range(GROUP):
                        src = part[HEAD * h:HEAD * (h + 1), buf, :].bitcast(F32)
                        if j < 2:
                            parity = (GROUPS * (fr.odd + off) + g) % 2
                            dst = k_stack[rows, parity, h, HALF * j:HALF * (j + 1)]
                        else:
                            dst = q_stack[rows, j - 2, h, :]
                        sp.dma_start(dst.bitcast(F32), src).then_inc(stacked[j], 16)

            def frame(fr, layer, next_layer):
                def rows(tensor, off, in_layer, t0, n, cols):
                    b = fr.count(1, off - BATCH * in_layer)
                    view = tensor.rearrange("b (t p) c -> p b t c", p=P)
                    return view[:, bass.ds(b, 1), t0:t0 + n, :].rearrange("p b t c -> p (b t) c")

                def x_rows(off, in_layer, t):
                    return rows(out if in_layer else x, off, in_layer, t, 1, HIDDEN)

                def stored_before(off, in_layer):
                    if in_layer:
                        for s in out_stored:
                            sp_wait(fr, s, fr.count(64, 64 * (off - BATCH + 1)))

                for n in range(fr.slots):
                    if fr.cur and n == 7:
                        sp_wait(fr, shared_filled, fr.turn("O", TILES - 1, -1) if fr.prev else 0)
                        sp_wait(fr, res_ready, fr.count(TILES, 0))
                        sp.dma_start(w_o[:], weights[layer, 3].rearrange("(k p) o -> p k o", p=P))\
                            .then_inc(wo_loaded, 16)
                        sp.dma_start(bias_o[:], biases[layer, 1].partition_broadcast(P)).then_inc(wo_loaded, 16)
                    if fr.next and n == 10:
                        sp_wait(fr, shared_drained, fr.turn("V", TILES - 1) if fr.cur else 0)
                        sp.dma_start(w_v[:], weights[next_layer, 2].rearrange("(k p) o -> p k o", p=P))\
                            .then_inc(wv_loaded, 16)
                        sp.dma_start(bias_v[:], biases[next_layer, 0].partition_broadcast(P)).then_inc(wv_loaded, 16)
                    if fr.next and n == 12:
                        sp_wait(fr, shifted_ready, fr.count(ITEMS, 0))
                        sp.dma_start(consts[:, 1 - fr.odd, :], layer_consts[next_layer]).then_inc(consts_loaded, 16)
                    if fr.next and SLOT_X - 2 <= n < SLOT_X - 2 + TILES:
                        t = n - SLOT_X + 2
                        if t == 0:
                            stored_before(1, next_layer)
                        if t >= 2:
                            sp_wait(fr, shared_filled, fr.turn("X", t - 2, 1))
                        elif fr.cur:
                            sp_wait(fr, shared_filled, fr.turn("X", TILES - 2 + t, 0))
                        sp.dma_start(x_in[:, t % 2:t % 2 + 1, :], x_rows(1, next_layer, t)).then_inc(x_loaded[t % 2], 16)
                    if fr.next and n == SLOT_X:
                        if fr.cur:
                            sp_wait(fr, shared_filled, fr.turn("P", 4 * GROUPS - 1))
                        for w in range(2):
                            sp.dma_start(w_qk[:, w], weights[next_layer, w].rearrange("(k p) o -> p k o", p=P))\
                                .then_inc(wqk_loaded, 16)
                    for t, slot in enumerate(SLOT_O):
                        off = -1 if slot - 4 >= ITEMS else 0
                        if (slot - 4) % ITEMS == n and fr.has(off):
                            if t == 0:
                                stored_before(off, layer)
                            sp_wait(fr, out_stored[t % 2], fr.count(64, 64 * off + 16 * (t // 2)))
                            in_layer = layer if off == 0 or fr.f != BATCH else 0
                            sp.dma_start(res[:, t % 2:t % 2 + 1, :], x_rows(off, in_layer, t)).then_inc(res_loaded[t % 2], 16)
                    for w in (1, 2):
                        for kind, index, off in fr.turns_at(n - 1, w):
                            if kind == "P":
                                stack_dmas(fr, index, off)
                    j = (n - 2 * ITEMS_OF_GROUP - CHUNK - 1) // CHUNK if n > ITEMS_OF_GROUP else -1
                    if n % CHUNK == 1 and (0 <= j < 3 and fr.next or n == 1 and fr.cur):
                        off = 1
                        if n == 1:
                            j, off = 3, 0
                        sp_wait(fr, shifted_ready, fr.count(ITEMS, ITEMS * off - ITEMS_OF_GROUP + CHUNK * (j + 1)))
                        in_layer = next_layer if off else layer
                        sp.dma_start(adj_sb[:, 2 * j:2 * j + 2, :], rows(adj, off, in_layer, 2 * j, 2, TOKENS))\
                            .then_inc(adj_loaded[j], 16)

            sp.dma_start(ident[:], identity).then_inc(ident_loaded, 16)
            frame(Frame(-1, 1), 0, 0)
            mid = BATCH // 2
            frame(Frame(0, 0), 0, 0)
            frame(Frame(0, 1), 0, 0)
            with sp.Fori(1, mid - 1) as pair:
                frame(Frame(pair, 0), 0, 0)
                frame(Frame(pair, 1), 0, 0)
            frame(Frame(mid - 1, 0), 0, 0)
            frame(Frame(mid - 1, 1), 0, 1)
            frame(Frame(mid, 0), 1, 1)
            frame(Frame(mid, 1), 1, 1)
            with sp.Fori(mid + 1, STEPS // 2 - 1) as pair:
                frame(Frame(pair, 0), 1, 1)
                frame(Frame(pair, 1), 1, 1)
            frame(Frame(STEPS // 2 - 1, 0), 1, 1)
            frame(Frame(STEPS // 2 - 1, 1), 1, 1)
            frame(Frame(STEPS // 2, 0), 1, 1)

        @block.tensor
        def _(pe):
            def project(fr, index, off):
                g, j = divmod(index, 4)
                is_key = j < 2
                if index == 0:
                    pe.wait_ge(wqk_loaded, fr.count(32, 32 * (off + 1)))
                wait(pe, shared_drained, fr.turn("P", index, off) - 1)
                for k in range(KT):
                    last = nc.tensor.matmul(ps_shared[:], w_qk[:, int(is_key), k, P * g:P * (g + 1)],
                                            x_turned[:, k, HALF * (j % 2):HALF * (j % 2 + 1)],
                                            start=(k == 0), stop=(k == KT - 1))
                last.then_inc(shared_filled, 1)

            def turn_x(fr, t, off):
                pe.wait_ge(x_loaded[t % 2], fr.count(64, 64 * off + 16 * (t // 2 + 1)))
                wait(pe, shared_drained, fr.turn("X", t, off) - 1)
                for k in range(KT):
                    last = nc.tensor.transpose(ps_shared[:, P * k:P * (k + 1)], x_in[:, t % 2, P * k:P * (k + 1)],
                                               ident[:])
                last.then_inc(shared_filled, 1)

            def make_values(fr, t):
                if t == 0:
                    pe.wait_ge(wv_loaded, fr.count(32, 32))
                wait(pe, shared_drained, fr.turn("V", t) - 1)
                for k in range(KT):
                    last = nc.tensor.matmul(ps_shared[:, 0:HIDDEN], x_turned[:, k, P * t:P * (t + 1)], w_v[:, k, :],
                                            start=(k == 0), stop=(k == KT - 1))
                last.then_inc(shared_filled, 1)

            def project_out(fr, t, off):
                if t == 0:
                    pe.wait_ge(wo_loaded, fr.count(32, 32 * (off + 1)))
                pe.wait_ge(out_moved, fr.count(CHUNKS, CHUNKS * off + 2 * CHUNKS_OF_GROUP + t // 2 + 1))
                wait(pe, shared_drained, fr.turn("O", t, off) - 1)
                for k in range(GROUPS):
                    last = nc.tensor.matmul(ps_shared[:, 0:HIDDEN], out_turned[:, k, P * t:P * (t + 1)], w_o[:, k, :],
                                            start=(k == 0), stop=(k == GROUPS - 1))
                last.then_inc(shared_filled, 1)

            def turn_inverse(fr, c, off):
                pe.wait_ge(wide_ready, fr.count(CHUNKS, CHUNKS * off + c + 1))
                wait(pe, shared_drained, fr.turn("R", c, off) - 1)
                for q in range(2):
                    last = nc.tensor.transpose(ps_shared[:, P * q:P * (q + 1)],
                                               inverse_wide[:, q].rearrange("p h d -> p (h d)"), ident[:])
                last.then_inc(shared_filled, 1)

            def scores(fr, n):
                g, h, qt = item_of(n)
                group = fr.count(GROUPS, g + 1)
                if n % ITEMS_OF_GROUP == 0:
                    for s in stacked[0:3]:
                        pe.wait_ge(s, group * (16 * 4 * GROUP))
                if n % ITEMS_OF_GROUP == ITEMS_OF_GROUP // 2:
                    pe.wait_ge(stacked[3], group * (16 * 4 * GROUP))
                wait(pe, shifted_ready, fr.count(ITEMS, n - 1))
                parity = (GROUPS * fr.odd + g) % 2
                for half in range(2):
                    last = nc.tensor.matmul(ps_scores[:, n % 2, HALF * half:HALF * (half + 1)],
                                            q_stack[:, qt // 4, h, P * (qt % 4):P * (qt % 4 + 1)],
                                            k_stack[:, parity, h, HALF * half:HALF * (half + 1)],
                                            start=True, stop=True)
                last.then_inc(scores_ready, 1)

            def turn_probs(fr, n, off):
                pe.wait_ge(probs_ready, fr.count(ITEMS, ITEMS * off + n + 1))
                for half, (moved, turned) in enumerate(((moved_a, turned_a), (moved_b, turned_b))):
                    wait(pe, moved, fr.count(ITEMS, ITEMS * off + n))
                    for k in range(TILES // 2):
                        last = nc.tensor.transpose(ps_turn[:, half, P * k:P * (k + 1)],
                                                   probs[:, n % RING, HALF * half + P * k:HALF * half + P * (k + 1)],
                                                   ident[:])
                    last.then_inc(turned, 1)

            def weighted_sum(fr, c, off):
                g = c // CHUNKS_OF_GROUP
                pe.wait_ge(moved_a, fr.count(ITEMS, ITEMS * off + CHUNK * (c + 1)))
                pe.wait_ge(moved_b, fr.count(ITEMS, ITEMS * off + CHUNK * (c + 1)))
                if c == 0:
                    pe.wait_ge(shared_drained, fr.turn("V", TILES - 1))
                wait(pe, out_moved, fr.count(CHUNKS, CHUNKS * off + c))
                for k in range(TILES):
                    for h in range(GROUP):
                        col = P * g + HEAD * h
                        last = nc.tensor.matmul(ps_out[HEAD * h:HEAD * (h + 1), 0:PAIR_Q], values[:, k, col:col + HEAD],
                                                probs_turned[:, 2 * h:2 * h + 2, k, :],
                                                start=(k == 0), stop=(k == TILES - 1))
                last.then_inc(pv_ready, 1)

            def shared_turns(fr, n, window):
                for kind, index, off in fr.turns_at(n, window):
                    if kind == "P":
                        project(fr, index, off)
                    if kind == "X":
                        turn_x(fr, index, off)
                    if kind == "V":
                        make_values(fr, index)
                    if kind == "O":
                        project_out(fr, index, off)
                    if kind == "R":
                        turn_inverse(fr, index, off)

            def frame(fr):
                for n in range(fr.slots):
                    if fr.cur:
                        scores(fr, n)
                    if n % CHUNK == 2:
                        item, off = before(n, CHUNK + 2)
                        if fr.has(off):
                            weighted_sum(fr, item // CHUNK, off)
                    shared_turns(fr, n, 1)
                    item, off = before(n, 2)
                    if fr.has(off) and (fr.cur or off == -1):
                        turn_probs(fr, item, off)
                    shared_turns(fr, n, 2)

            pe.wait_ge(ident_loaded, 16)
            run_frames(pe, frame)

        @block.scalar
        def _(act):
            def split_hi(fr, index, off):
                j = index % 4
                group = fr.count(GROUPS, GROUPS * off + index // 4)
                act.wait_ge(shared_filled, fr.turn("P", index, off))
                wait(act, stacked[(j + 2) % 4], (group + (1 if j >= 2 else 0)) * (16 * 4 * GROUP))
                if j == 2:
                    act.wait_ge(consts_loaded, fr.count(16, 16 * (off + 1)))
                scale = 1.0 if j < 2 else consts[:, (fr.odd + off) % 2, 1:2]
                nc.scalar.activation(part_hi[:, j % 2, :], ps_shared[:], ACT.Identity, scale=scale)\
                    .then_inc(hi_ready, 1)

            def move_x(fr, t, off):
                act.wait_ge(shared_filled, fr.turn("X", t, off))
                nc.scalar.activation(x_turned[:, :, P * t:P * (t + 1)],
                                     ps_shared[:, 0:HIDDEN].rearrange("p (k c) -> p k c", k=KT), ACT.Copy)\
                    .then_inc(shared_drained, 1)

            def move_inverse(fr, c, off):
                act.wait_ge(shared_filled, fr.turn("R", c, off))
                wait(act, out_moved, fr.count(CHUNKS, CHUNKS * off + c))
                nc.scalar.activation(inverse_turned[:], ps_shared[:, 0:PAIR_Q], ACT.Copy).then_inc(shared_drained, 1)

            def exponentials(fr, n):
                c = n // CHUNK
                act.wait_ge(shifted_ready, fr.count(ITEMS, n + 1))
                if n % CHUNK == 0:
                    wait(act, wide_ready, fr.count(CHUNKS, c - 1))
                col = n % CHUNK
                nc.scalar.activation(probs[:, n % RING, :], probs[:, n % RING, :], ACT.Exp,
                                     bias=neg_max[:, c % 2, col:col + 1], scale=-1.0,
                                     accum_out=row_sum[:, c % 2, col:col + 1]).then_inc(probs_ready, 1)

            def move_turned(fr, n, off):
                act.wait_ge(turned_a, fr.count(ITEMS, ITEMS * off + n + 1))
                if n % CHUNK == 0:
                    wait(act, pv_ready, fr.count(CHUNKS, CHUNKS * off + n // CHUNK))
                nc.scalar.activation(probs_turned[:, n % CHUNK, 0:TILES // 2, :],
                                     ps_turn[:, 0, :].rearrange("p (k q) -> p k q", q=P), ACT.Copy)\
                    .then_inc(moved_a, 1)

            def shared_turns(fr, n, window):
                for kind, index, off in fr.turns_at(n, window):
                    if kind == "P":
                        split_hi(fr, index, off)
                    if kind == "X":
                        move_x(fr, index, off)
                    if kind == "R":
                        move_inverse(fr, index, off)

            def frame(fr):
                for n in range(fr.slots):
                    shared_turns(fr, n, 1)
                    item, off = before(n, 2)
                    if fr.has(off) and (fr.cur or off == -1):
                        move_turned(fr, item, off)
                    if fr.cur:
                        exponentials(fr, n)
                    shared_turns(fr, n, 2)

            run_frames(act, frame)

        @block.vector
        def _(dve):
            def shift(fr, n):
                c = n // CHUNK
                g, h, qt = item_of(n)
                if n == 0:
                    dve.wait_ge(consts_loaded, fr.count(16, 16))
                if g == 0 and n % CHUNK == 0:
                    dve.wait_ge(adj_loaded[c], fr.count(16, 16))
                if n % CHUNK == 0:
                    wait(dve, wide_ready, fr.count(CHUNKS, c - 1))
                dve.wait_ge(scores_ready, fr.count(ITEMS, n + 1))
                wait(dve, turned_b, fr.count(ITEMS, n + 1 - RING))
                settle(dve, fr, dve_settled)
                col = n % CHUNK
                nc.vector.tensor_tensor_reduce(out=probs[:, n % RING, :], in0=ps_scores[:, n % 2, :],
                                               in1=adj_sb[:, qt, :], scale=consts[:, fr.odd, 0:1], scalar=3.0e38,
                                               op0=ALU.add, op1=ALU.min,
                                               accum_out=neg_max[:, c % 2, col:col + 1]).then_inc(shifted_ready, 1)

            def invert(fr, c, off):
                dve.wait_ge(probs_ready, fr.count(ITEMS, ITEMS * off + CHUNK * (c + 1)))
                wait(dve, wide_ready, fr.count(CHUNKS, CHUNKS * off + c - 1))
                nc.vector.reciprocal(inverse[:, c % 2, :], row_sum[:, c % 2, :]).then_inc(inverse_ready, 1)

            def split_lo(fr, index, off):
                j = index % 4
                dve.wait_ge(hi_ready, fr.count(4 * GROUPS, 4 * GROUPS * off + index + 1))
                hi = part_hi[:, j % 2, :].bitcast(F32)
                if j < 2:
                    ins = nc.vector.tensor_tensor(part_lo[:, j % 2, :], ps_shared[:], hi, ALU.subtract)
                else:
                    ins = nc.vector.scalar_tensor_tensor(part_lo[:, j % 2, :], ps_shared[:],
                                                         consts[:, (fr.odd + off) % 2, 1:2], hi,
                                                         ALU.mult, ALU.subtract)
                ins.then_inc(shared_drained, 1)

            def move_values(fr, t):
                if t == 0:
                    dve.wait_ge(wv_loaded, fr.count(32, 32))
                dve.wait_ge(shared_filled, fr.turn("V", t))
                nc.vector.tensor_tensor(values[:, t, :], ps_shared[:, 0:HIDDEN], bias_v[:], ALU.add)\
                    .then_inc(shared_drained, 1)

            def move_turned(fr, n, off):
                dve.wait_ge(turned_b, fr.count(ITEMS, ITEMS * off + n + 1))
                if n % CHUNK == 0:
                    wait(dve, pv_ready, fr.count(CHUNKS, CHUNKS * off + n // CHUNK))
                nc.vector.tensor_copy(probs_turned[:, n % CHUNK, TILES // 2:TILES, :],
                                      ps_turn[:, 1, :].rearrange("p (k q) -> p k q", q=P)).then_inc(moved_b, 1)

            def normalise(fr, c, off):
                g, q0 = c // CHUNKS_OF_GROUP, PAIR_Q * (c % CHUNKS_OF_GROUP)
                dve.wait_ge(pv_ready, fr.count(CHUNKS, CHUNKS * off + c + 1))
                dve.wait_ge(shared_drained, fr.turn("R", c, off))
                nc.vector.tensor_tensor(out_turned[:, g, q0:q0 + PAIR_Q], ps_out[:, 0:PAIR_Q], inverse_turned[:],
                                        ALU.mult).then_inc(out_moved, 1)

            def residual(fr, t, off):
                done = fr.count(TILES, TILES * off + t + 1)
                dve.wait_ge(shared_filled, fr.turn("O", t, off))
                dve.wait_ge(res_ready, done)
                nc.vector.tensor_tensor(res[:, t % 2, :], ps_shared[:, 0:HIDDEN], res[:, t % 2, :], ALU.add)\
                    .then_inc(shared_drained, 1)
                dve.wait_ge(shared_drained, fr.turn("O", t, off))
                nc.vector.bn_stats(stats[:, t % 2, :], res[:, t % 2, :]).then_inc(stats_step, 1)
                dve.wait_ge(stats_step, done)
                settle(dve, fr, dve_settled)
                nc.vector.bn_aggr(mean_var[:, t % 2, :], stats[:, t % 2, :]).then_inc(stats_ready, 1)

            def shared_turns(fr, n, window):
                for kind, index, off in fr.turns_at(n, window):
                    if kind == "P":
                        split_lo(fr, index, off)
                    if kind == "V":
                        move_values(fr, index)
                    if kind == "O":
                        residual(fr, index, off)

            def frame(fr):
                for n in range(fr.slots):
                    if fr.cur:
                        shift(fr, n)
                    item, off = before(n, CHUNK + 1)
                    if n % CHUNK == 1 and fr.has(off) and (fr.cur or off == -1):
                        invert(fr, item // CHUNK, off)
                    shared_turns(fr, n, 1)
                    item, off = before(n, 2)
                    if fr.has(off) and (fr.cur or off == -1):
                        move_turned(fr, item, off)
                    item, off = before(n, CHUNK + 2)
                    if n % CHUNK == 2 and fr.has(off) and (fr.cur or off == -1):
                        normalise(fr, item // CHUNK, off)
                    shared_turns(fr, n, 2)

            run_frames(dve, frame)

        @block.gpsimd
        def _(pool):
            GUARD_STEPS, NORM_STEPS = 5, 3

            def widen(fr, c, off):
                base = fr.count(CHUNKS, CHUNKS * off + c) * GUARD_STEPS
                ones, zero_max, keep = (guard[:, i, :] for i in range(3))
                pool.wait_ge(inverse_ready, fr.count(CHUNKS, CHUNKS * off + c + 1))
                settle(pool, fr, pool_settled)
                nc.gpsimd.tensor_scalar(ones, row_sum[:, c % 2, :], float(TOKENS), -1.0, ALU.is_equal, ALU.mult)\
                    .then_inc(guard_step, 1)
                settle(pool, fr, pool_settled)
                nc.gpsimd.tensor_scalar(zero_max, neg_max[:, c % 2, :], 0.0, None, ALU.is_equal)\
                    .then_inc(guard_step, 1)
                pool.wait_ge(guard_step, base + 2)
                nc.gpsimd.tensor_tensor(keep, ones, zero_max, ALU.mult).then_inc(guard_step, 1)
                pool.wait_ge(guard_step, base + 3)
                settle(pool, fr, pool_settled)
                nc.gpsimd.tensor_scalar(ones, keep, 1.0, None, ALU.add).then_inc(guard_step, 1)
                pool.wait_ge(guard_step, base + 4)
                nc.gpsimd.tensor_tensor(keep, ones, inverse[:, c % 2, :], ALU.mult).then_inc(guard_step, 1)
                pool.wait_ge(guard_step, base + 5)
                if c > 0:
                    wait(pool, shared_filled, fr.turn("R", c - 1, off))
                elif fr.prev:
                    wait(pool, shared_filled, fr.turn("R", CHUNKS - 1, off - 1))
                settle(pool, fr, pool_settled)
                nc.gpsimd.tensor_copy(inverse_wide[:],
                                      keep.rearrange("p (h q) -> p q h", q=2).unsqueeze(3)
                                      .broadcast_to([P, 2, GROUP, HEAD])).then_inc(wide_ready, 1)

            def add_bias(fr, t, off):
                if t == 0:
                    pool.wait_ge(wo_loaded, fr.count(32, 32 * (off + 1)))
                pool.wait_ge(res_loaded[t % 2], fr.count(64, 64 * off + 16 * (t // 2 + 1)))
                nc.gpsimd.tensor_tensor(res[:, t % 2, :], res[:, t % 2, :], bias_o[:], ALU.add).then_inc(res_ready, 1)

            def layernorm(fr, t, off):
                base = fr.count(TILES, TILES * off + t) * NORM_STEPS
                pool.wait_ge(stats_ready, fr.count(TILES, TILES * off + t + 1))
                settle(pool, fr, pool_settled)
                nc.gpsimd.tensor_scalar(rstd[:, t % 2, 0:1], mean_var[:, t % 2, 1:2], EPS, None, ALU.add)\
                    .then_inc(norm_step, 1)
                pool.wait_ge(norm_step, base + 1)
                nc.gpsimd.tensor_tensor(rstd[:, t % 2, 1:2], rstd[:, t % 2, 0:1], minus_half[:], ALU.pow)\
                    .then_inc(norm_step, 1)
                pool.wait_ge(norm_step, base + 2)
                settle(pool, fr, pool_settled)
                nc.gpsimd.tensor_scalar(res[:, t % 2, :], res[:, t % 2, :], mean_var[:, t % 2, 0:1],
                                        rstd[:, t % 2, 1:2], ALU.subtract, ALU.mult).then_inc(norm_step, 1)
                pool.wait_ge(norm_step, base + 3)
                rows = out.rearrange("s (t p) c -> p s t c", p=P)[:, bass.ds(fr.count(1, off), 1), t, :]
                pool.dma_start(rows, res[:, t % 2:t % 2 + 1, :]).then_inc(out_stored[t % 2], 16)

            def frame(fr):
                for n in range(fr.slots):
                    item, off = before(n, CHUNK + 1)
                    if n % CHUNK == 1 and fr.has(off) and (fr.cur or off == -1):
                        widen(fr, item // CHUNK, off)
                    for t, slot in enumerate(SLOT_O):
                        for at, program in ((slot - 2, add_bias), (slot + 1, layernorm)):
                            if at % ITEMS == n and fr.has(-(at // ITEMS)):
                                program(fr, t, -(at // ITEMS))

            nc.gpsimd.memset(minus_half[:], -0.5).then_inc(half_set, 1)
            pool.wait_ge(half_set, 1)
            run_frames(pool, frame)
            for s in out_stored:
                pool.wait_ge(s, 16 * STEPS * TILES // 2)


def kernel(x, adj, L0_gnn_Wq, L0_gnn_Wk, L0_gnn_Wv, L0_gnn_bv, L0_gnn_Wo, L0_gnn_bo,
           L1_gnn_Wq, L1_gnn_Wk, L1_gnn_Wv, L1_gnn_bv, L1_gnn_Wo, L1_gnn_bo):
    import numpy as np
    import concourse.bacc as bacc
    from concourse.bass_utils import run_bass_kernel_spmd

    weights = np.stack([np.stack([np.asarray(w).T for w in layer]) for layer in
                        ((L0_gnn_Wq, L0_gnn_Wk, L0_gnn_Wv, L0_gnn_Wo), (L1_gnn_Wq, L1_gnn_Wk, L1_gnn_Wv, L1_gnn_Wo))])
    biases = np.stack([np.stack([np.asarray(b) for b in layer]) for layer in
                       ((L0_gnn_bv, L0_gnn_bo), (L1_gnn_bv, L1_gnn_bo))])
    layer_consts = np.array([[[-f, SCALE / f]] * P for f in (2.0, 1.0)], np.float32)
    arrays = {"x": np.asarray(x), "adj": np.asarray(adj), "weights": np.ascontiguousarray(weights),
              "biases": np.ascontiguousarray(biases), "layer_consts": layer_consts,
              "identity": np.eye(P, dtype=np.float32)}
    nc = bacc.Bacc("TRN2", target_bir_lowering=False, num_devices=1)
    args = [nc.dram_tensor(f"in_{n}", a.shape, mybir.dt.from_np(a.dtype), kind="ExternalInput").ap()
            for n, a in arrays.items()]
    out = nc.dram_tensor("out", (STEPS, TOKENS, HIDDEN), F32, kind="ExternalOutput").ap()
    build(nc, *args, out)
    r = run_bass_kernel_spmd(nc, [{f"in_{n}": a for n, a in arrays.items()}], core_ids=[0])
    return r.results[0]["out"][BATCH:]
```

```python
from contextlib import ExitStack

import concourse.bass as bass
from concourse import mybir

P = 128
LAYERS, BATCH, TOKENS, HIDDEN, HEADS = 2, 8, 1024, 384, 12
HEAD = HIDDEN // HEADS
STEPS = LAYERS * BATCH
KT = HIDDEN // P
TILES = TOKENS // P
GROUP = P // HEAD
GROUPS = HEADS // GROUP
HALF = TOKENS // 2
CHUNK = 2 * GROUP
CHUNKS = GROUPS * TILES // 2
CHUNKS_OF_GROUP = CHUNKS // GROUPS
ITEMS = CHUNKS * CHUNK
ITEMS_OF_GROUP = ITEMS // GROUPS
PAIR_Q = 2 * P
RING = 3
EPS = 1e-5
SCALE = float(HIDDEN) ** -0.5

F32 = mybir.dt.float32
F32R = mybir.dt.float32r
ACT = mybir.ActivationFunctionType
ALU = mybir.AluOpType

PT_RING = 12
PIECES = 4
PIECE = TILES // PIECES
SLOT_SUM = CHUNK + 3
SLOT_NORM = SLOT_SUM + PIECES - 1

TIMETABLE = {("V", t): [(6 + t, 2)] * 3 for t in range(TILES)}
TIMETABLE |= {("X", t): [(slot - ITEMS, window)] for t, (slot, window) in enumerate((
    (49, 2), (50, 1), (54, 1), (54, 2), (59, 1), (60, 1), (63, 1), (64, 1)))}
TIMETABLE |= {("O", t): at for t, at in enumerate((
    [(79, 2), (80, 1), (80, 2)], [(81, 2), (82, 1), (82, 2)], [(89, 2), (90, 1), (90, 2)],
    [(95, 1), (95, 2), (95, 2)], [(111, 1), (111, 2), (112, 1)], [(121, 1), (121, 2), (122, 1)],
    [(127, 1), (127, 2), (128, 1)], [(129, 1), (129, 2), (130, 1)]))}
TIMETABLE |= {("P", n): at for n, at in enumerate((
    [(64 - ITEMS, 2), (65 - ITEMS, 1), (66 - ITEMS, 1)], [(73 - ITEMS, 1), (73 - ITEMS, 2), (74 - ITEMS, 1)],
    [(71 - ITEMS, 1), (71 - ITEMS, 2), (72 - ITEMS, 1)], [(87 - ITEMS, 1), (87 - ITEMS, 2), (88 - ITEMS, 1)],
    [(0, 2), (1, 1), (1, 2)], [(17, 1), (17, 2), (18, 1)],
    [(23, 1), (23, 2), (24, 1)], [(39, 1), (39, 2), (40, 1)],
    [(41, 1), (41, 2), (42, 1)], [(55, 1), (55, 2), (56, 1)],
    [(47, 1), (47, 2), (48, 1)], [(57, 1), (57, 2), (58, 1)]))}
PROJECTED = sorted(range(4 * GROUPS), key=lambda n: TIMETABLE["P", n])
SLOT_STACK = [-28, -21, -16, 0, 3, 19, 25, 41, 43, 57, 52, 64]
SLOT_RES = [74, 76, 85, 88, 105, 115, 121, 126]
SLOT_BIAS = [77, 78, 88, 93, 108, 118, 124, 128]
SLOT_X = [38, 38, 51, 51, 56, 56, 61, 61]
SLOT_W_V, SLOT_W_QK = 59 - ITEMS, [43 - ITEMS, 91 - ITEMS, 14]
TAIL = 38


def turns_of_frame():
    turns = []
    for (kind, index), pieces in TIMETABLE.items():
        off = -(pieces[0][0] // ITEMS)
        assert pieces[-1][0] // ITEMS == -off
        turns.append(([(slot + ITEMS * off, window) for slot, window in pieces], kind, index, off))
    turns.sort()
    assert all(a[0][-1] <= b[0][0] for a, b in zip(turns, turns[1:]))
    return turns


TURNS = turns_of_frame()
BEFORE = sum(1 for t in TURNS if t[3] == 1) - sum(1 for t in TURNS if t[3] == -1)


class Frame:

    def __init__(self, pair, odd, first=0, last=0):
        self.pair, self.odd = pair, odd
        self.f = 2 * pair + odd if isinstance(pair, int) else None
        f = self.f
        self.prev = f is None or f > 0
        self.cur = f is None or 0 <= f < STEPS
        self.next = f is None or f < STEPS - 1
        self.slots = ITEMS if f is None or f < STEPS else TAIL

    def count(self, per_step, n):
        return self.pair * (2 * per_step) + (self.odd * per_step + n)

    def has(self, off):
        return (self.prev, self.cur, self.next)[off + 1]

    def turn(self, kind, index, off=0):
        at = next(n for n, t in enumerate(TURNS) if t[1] == kind and t[2] == index)
        frame_off = off - TURNS[at][3]
        if self.f is None:
            return self.count(len(TURNS), frame_off * len(TURNS) + BEFORE + at + 1)
        return sum(1 for f in range(-1, self.f + frame_off + 1)
                   for t in (TURNS if f < self.f + frame_off else TURNS[:at + 1]) if 0 <= f + t[3] < STEPS)

    def pieces_at(self, slot, window):
        found = []
        for pieces, kind, index, off in TURNS:
            here = [n for n, at in enumerate(pieces) if at == (slot, window)]
            if here and self.has(off):
                found.append((kind, index, off, here, len(pieces)))
        return found

    def turns_at(self, slot, window):
        return [(k, i, off) for k, i, off, here, n in self.pieces_at(slot, window) if n - 1 in here]


STACK_LAG = (ITEMS_OF_GROUP, ITEMS_OF_GROUP, ITEMS_OF_GROUP // 2, 0)
assert all(slot >= max(TIMETABLE["P", n][-1][0] + 1, ITEMS_OF_GROUP * (n // 4) - STACK_LAG[n % 4])
           for n, slot in enumerate(SLOT_STACK))


def wait(eng, sem, value):
    if not (isinstance(value, int) and value <= 0):
        eng.wait_ge(sem, value)


def settle(eng, fr, counter):
    if fr.f is None:
        eng.sem_inc(counter, 1)


def run_frames(eng, frame_program):
    frame_program(Frame(-1, 1))
    frame_program(Frame(0, 0))
    frame_program(Frame(0, 1))
    with eng.Fori(1, STEPS // 2 - 1) as pair:
        frame_program(Frame(pair, 0))
        frame_program(Frame(pair, 1))
    frame_program(Frame(STEPS // 2 - 1, 0))
    frame_program(Frame(STEPS // 2 - 1, 1))
    frame_program(Frame(STEPS // 2, 0))


def item_of(n):
    chunk = n // CHUNK
    return chunk // CHUNKS_OF_GROUP, (n % CHUNK) // 2, 2 * (chunk % CHUNKS_OF_GROUP) + n % 2


def before(n, lag):
    return (n - lag, 0) if n >= lag else (n - lag + ITEMS, -1)


def build(nc, x, adj, weights, biases, layer_consts, identity, out):
    ctx = ExitStack()
    with ctx:
        def sb(name, shape, dt=F32):
            return ctx.enter_context(nc.sbuf_tensor(name, shape, dt))

        def psum(name, shape):
            return ctx.enter_context(nc.psum_tensor(name, shape, F32))

        def sem(name):
            return ctx.enter_context(nc.semaphore(name))

        ident = sb("ident", [P, P])
        x_in = sb("x_in", [P, 2, HIDDEN])
        x_turned = sb("x_turned", [P, KT, TOKENS])
        w_even = sb("w_even", [P, 2, KT, P])
        w_odd = sb("w_odd", [P, KT * HIDDEN])
        w_v = w_odd[:].rearrange("p (k c) -> p k c", k=KT)
        w_qk = (w_even[:], w_even[:], w_odd[:, 0:2 * KT * P].rearrange("p (w k c) -> p w k c", w=2, k=KT))
        w_o = sb("w_o", [P, KT, HIDDEN])
        bias_v = sb("bias_v", [P, HIDDEN])
        bias_o = sb("bias_o", [P, HIDDEN])
        factors = sb("factors", [P, 5])
        consts = factors[:, 0:4].rearrange("p (b i) -> p b i", b=2)
        minus_half = factors[:, 4:5]
        part_hi = sb("part_hi", [P, 2, HALF], F32R)
        part_lo = sb("part_lo", [P, 2, HALF], F32R)
        k_stack = sb("k_stack", [P, 2, GROUP, TOKENS], F32R)
        q_stack = sb("q_stack", [P, 2, GROUP, HALF], F32R)
        adj_sb = sb("adj_sb", [P, TILES, TOKENS])
        probs = sb("probs", [P, RING, TOKENS])
        neg_max = sb("neg_max", [P, 2, CHUNK])
        row_sum = sb("row_sum", [P, 2, CHUNK])
        inverse = sb("inverse", [P, 2, CHUNK])
        guard = sb("guard", [P, 2, CHUNK])
        inverse_wide = sb("inverse_wide", [P, 2, GROUP, HEAD])
        inverse_turned = sb("inverse_turned", [P, PAIR_Q])
        probs_turned = sb("probs_turned", [P, PT_RING, TILES, P])
        values = sb("values", [P, TILES, HIDDEN])
        out_turned = sb("out_turned", [P, GROUPS, TOKENS])
        res = sb("res", [P, 2, HIDDEN])
        layer_stats = sb("layer_stats", [P, 2, 8])
        stats = layer_stats[:, :, 0:6]
        mean_var = layer_stats[:, :, 6:8]

        ps_scores = psum("ps_scores", [P, 2, TOKENS])
        ps_turn = psum("ps_turn", [P, 2, HALF])
        ps_out = psum("ps_out", [P, HALF])
        ps_shared = psum("ps_shared", [P, HALF])

        ident_loaded = sem("ident_loaded")
        x_loaded = [sem(f"x_loaded{i}") for i in range(2)]
        w_even_loaded, w_odd_loaded = sem("w_even_loaded"), sem("w_odd_loaded")
        wo_loaded = sem("wo_loaded")
        consts_loaded = sem("consts_loaded")
        stacked = [sem(f"stacked_{n}") for n in ("k0", "k1", "q0", "q1")]
        adj_loaded = [sem(f"adj_loaded{j}") for j in range(TILES // 2)]
        res_loaded = [sem(f"res_loaded{i}") for i in range(2)]
        shared_filled = sem("shared_filled")
        shared_drained = sem("shared_drained")
        hi_ready = sem("hi_ready")
        scores_ready = sem("scores_ready")
        shifted_ready = sem("shifted_ready")
        probs_ready = sem("probs_ready")
        turned_a = sem("turned_a")
        turned_b = sem("turned_b")
        moved_a = sem("moved_a")
        moved_b = sem("moved_b")
        pv_ready = sem("pv_ready")
        out_moved = sem("out_moved")
        inverse_filled = sem("inverse_filled")
        inverse_moved = sem("inverse_moved")
        inverse_ready = sem("inverse_ready")
        guard_step = sem("guard_step")
        wide_ready = sem("wide_ready")
        res_ready = sem("res_ready")
        stats_step = sem("stats_step")
        stats_ready = sem("stats_ready")
        norm_step = sem("norm_step")
        half_set = sem("half_set")
        out_stored = [sem(f"out_stored{i}") for i in range(2)]

        sp_settled, dve_settled, pool_settled = sem("sp_settled"), sem("dve_settled"), sem("pool_settled")

        block = ctx.enter_context(nc.Block())

        @block.sync
        def _(sp):
            def sp_wait(fr, sem, value):
                wait(sp, sem, value)
                settle(sp, fr, sp_settled)

            def stack_dmas(fr, index, off):
                g, j = divmod(index, 4)
                buf = j // 2
                group = fr.count(GROUPS, GROUPS * off + g)
                sp_wait(fr, shared_drained, fr.turn("P", index, off))
                sp_wait(fr, scores_ready, fr.count(ITEMS, ITEMS * off + ITEMS_OF_GROUP * g - STACK_LAG[j]))
                for block_row in range(4):
                    low = block_row % 2 if j >= 2 else block_row // 2
                    part = part_lo if low else part_hi
                    rows = slice(HEAD * block_row, HEAD * (block_row + 1))
                    for h in range(GROUP):
                        src = part[HEAD * h:HEAD * (h + 1), buf, :].bitcast(F32)
                        if j < 2:
                            parity = (GROUPS * (fr.odd + off) + g) % 2
                            dst = k_stack[rows, parity, h, HALF * j:HALF * (j + 1)]
                        else:
                            dst = q_stack[rows, j - 2, h, :]
                        sp.dma_start(dst.bitcast(F32), src).then_inc(stacked[j], 16)

            def frame(fr, layer, next_layer):
                def rows(tensor, off, in_layer, t0, n, cols):
                    b = fr.count(1, off - BATCH * in_layer)
                    view = tensor.rearrange("b (t p) c -> p b t c", p=P)
                    return view[:, bass.ds(b, 1), t0:t0 + n, :].rearrange("p b t c -> p (b t) c")

                def x_rows(off, in_layer, t):
                    return rows(out if in_layer else x, off, in_layer, t, 1, HIDDEN)

                def stored_before(off, in_layer):
                    if in_layer:
                        for s in out_stored:
                            sp_wait(fr, s, fr.count(64, 64 * (off - BATCH + 1)))

                for n in range(fr.slots):
                    if fr.cur and n == TAIL - 2:
                        if fr.prev:
                            sp_wait(fr, shared_filled, fr.turn("O", TILES - 1, -1))
                        sp_wait(fr, res_ready, fr.count(TILES, 0))
                        sp.dma_start(w_o[:], weights[layer, 3].rearrange("(k p) o -> p k o", p=P))\
                            .then_inc(wo_loaded, 16)
                        sp.dma_start(bias_o[:], biases[layer, 1].partition_broadcast(P)).then_inc(wo_loaded, 16)
                    if fr.next and n == SLOT_W_V + ITEMS:
                        if fr.cur:
                            sp_wait(fr, shared_filled, fr.turn("P", PROJECTED[-1]))
                        sp.dma_start(w_v, weights[next_layer, 2].rearrange("(k p) o -> p k o", p=P))\
                            .then_inc(w_odd_loaded, 16)
                        sp.dma_start(bias_v[:], biases[next_layer, 0].partition_broadcast(P))\
                            .then_inc(w_odd_loaded, 16)
                    for g, slot in enumerate(SLOT_W_QK):
                        off = -(slot // ITEMS)
                        if n == slot % ITEMS and fr.has(off):
                            if g == 2:
                                sp_wait(fr, shared_filled, fr.turn("V", TILES - 1))
                            elif g == 1:
                                sp_wait(fr, shared_filled, fr.turn("P", 3, 1))
                            elif fr.cur:
                                sp_wait(fr, shared_filled, fr.turn("P", 7))
                            for w in range(2):
                                src = weights[next_layer if off else layer, w].rearrange("(k p) o -> p k o", p=P)
                                sp.dma_start(w_qk[g][:, w], src[:, :, P * g:P * (g + 1)])\
                                    .then_inc(w_odd_loaded if g == 2 else w_even_loaded, 16)
                    if fr.next and n == 12:
                        sp_wait(fr, shifted_ready, fr.count(ITEMS, 0))
                        sp.dma_start(consts[:, 1 - fr.odd, :], layer_consts[next_layer]).then_inc(consts_loaded, 16)
                    for t in range(TILES):
                        if fr.next and n == SLOT_X[t]:
                            if t == 0:
                                stored_before(1, next_layer)
                            if t >= 2:
                                sp_wait(fr, shared_filled, fr.turn("X", t - 2, 1))
                            elif fr.cur:
                                sp_wait(fr, shared_filled, fr.turn("X", TILES - 2 + t, 0))
                            sp.dma_start(x_in[:, t % 2:t % 2 + 1, :], x_rows(1, next_layer, t))\
                                .then_inc(x_loaded[t % 2], 16)
                    for t, slot in enumerate(SLOT_RES):
                        off = -(slot // ITEMS)
                        if slot % ITEMS == n and fr.has(off):
                            if t == 0:
                                stored_before(off, layer)
                            sp_wait(fr, out_stored[t % 2], fr.count(64, 64 * off + 16 * (t // 2)))
                            in_layer = layer if off == 0 or fr.f != BATCH else 0
                            sp.dma_start(res[:, t % 2:t % 2 + 1, :], x_rows(off, in_layer, t)).then_inc(res_loaded[t % 2], 16)
                    for index, slot in enumerate(SLOT_STACK):
                        off = -(slot // ITEMS)
                        if slot % ITEMS == n and fr.has(off):
                            stack_dmas(fr, index, off)
                    j = (n - 2 * ITEMS_OF_GROUP - CHUNK - 1) // CHUNK if n > ITEMS_OF_GROUP else -1
                    if n % CHUNK == 1 and (0 <= j < 3 and fr.next or n == 1 and fr.cur):
                        off = 1
                        if n == 1:
                            j, off = 3, 0
                        sp_wait(fr, shifted_ready, fr.count(ITEMS, ITEMS * off - ITEMS_OF_GROUP + CHUNK * (j + 1)))
                        in_layer = next_layer if off else layer
                        sp.dma_start(adj_sb[:, 2 * j:2 * j + 2, :], rows(adj, off, in_layer, 2 * j, 2, TOKENS))\
                            .then_inc(adj_loaded[j], 16)

            sp.dma_start(ident[:], identity).then_inc(ident_loaded, 16)
            frame(Frame(-1, 1), 0, 0)
            mid = BATCH // 2
            frame(Frame(0, 0), 0, 0)
            frame(Frame(0, 1), 0, 0)
            with sp.Fori(1, mid - 1) as pair:
                frame(Frame(pair, 0), 0, 0)
                frame(Frame(pair, 1), 0, 0)
            frame(Frame(mid - 1, 0), 0, 0)
            frame(Frame(mid - 1, 1), 0, 1)
            frame(Frame(mid, 0), 1, 1)
            frame(Frame(mid, 1), 1, 1)
            with sp.Fori(mid + 1, STEPS // 2 - 1) as pair:
                frame(Frame(pair, 0), 1, 1)
                frame(Frame(pair, 1), 1, 1)
            frame(Frame(STEPS // 2 - 1, 0), 1, 1)
            frame(Frame(STEPS // 2 - 1, 1), 1, 1)
            frame(Frame(STEPS // 2, 0), 1, 1)

        @block.tensor
        def _(pe):
            def project(fr, index, off, here):
                g, j = divmod(index, 4)
                is_key = j < 2
                if 0 in here:
                    if j == 0:
                        pe.wait_ge((w_even_loaded, w_even_loaded, w_odd_loaded)[g],
                                   fr.count(64, 64 * off + (32, 64, 64)[g]))
                    wait(pe, shared_drained, fr.turn("P", index, off) - 1)
                for k in here:
                    last = nc.tensor.matmul(ps_shared[:], w_qk[g][:, int(is_key), k, :],
                                            x_turned[:, k, HALF * (j % 2):HALF * (j % 2 + 1)],
                                            start=(k == 0), stop=(k == KT - 1))
                return last

            def turn_x(fr, t, off):
                pe.wait_ge(x_loaded[t % 2], fr.count(64, 64 * off + 16 * (t // 2 + 1)))
                wait(pe, shared_drained, fr.turn("X", t, off) - 1)
                for k in range(KT):
                    last = nc.tensor.transpose(ps_shared[:, P * k:P * (k + 1)], x_in[:, t % 2, P * k:P * (k + 1)],
                                               ident[:])
                return last

            def make_values(fr, t, here):
                if 0 in here:
                    if t == 0:
                        pe.wait_ge(w_odd_loaded, fr.count(64, 32))
                    wait(pe, shared_drained, fr.turn("V", t) - 1)
                for k in here:
                    last = nc.tensor.matmul(ps_shared[:, 0:HIDDEN], x_turned[:, k, P * t:P * (t + 1)], w_v[:, k, :],
                                            start=(k == 0), stop=(k == KT - 1))
                return last

            def project_out(fr, t, off, here):
                if 0 in here:
                    if t == 0:
                        pe.wait_ge(wo_loaded, fr.count(32, 32 * (off + 1)))
                    pe.wait_ge(out_moved, fr.count(CHUNKS, CHUNKS * off + 2 * CHUNKS_OF_GROUP + t // 2 + 1))
                    wait(pe, shared_drained, fr.turn("O", t, off) - 1)
                for k in here:
                    last = nc.tensor.matmul(ps_shared[:, 0:HIDDEN], out_turned[:, k, P * t:P * (t + 1)], w_o[:, k, :],
                                            start=(k == 0), stop=(k == GROUPS - 1))
                return last

            def turn_inverse(fr, c, off):
                pe.wait_ge(wide_ready, fr.count(CHUNKS, CHUNKS * off + c + 1))
                for q in range(2):
                    last = nc.tensor.transpose(ps_out[:, PAIR_Q + P * q:PAIR_Q + P * (q + 1)],
                                               inverse_wide[:, q].rearrange("p h d -> p (h d)"), ident[:])
                last.then_inc(inverse_filled, 1)

            def scores(fr, n):
                g, h, qt = item_of(n)
                group = fr.count(GROUPS, g + 1)
                if n % ITEMS_OF_GROUP == 0:
                    for s in stacked[0:3]:
                        pe.wait_ge(s, group * (16 * 4 * GROUP))
                if n % ITEMS_OF_GROUP == ITEMS_OF_GROUP // 2:
                    pe.wait_ge(stacked[3], group * (16 * 4 * GROUP))
                wait(pe, shifted_ready, fr.count(ITEMS, n - 1))
                parity = (GROUPS * fr.odd + g) % 2
                for half in range(2):
                    last = nc.tensor.matmul(ps_scores[:, n % 2, HALF * half:HALF * (half + 1)],
                                            q_stack[:, qt // 4, h, P * (qt % 4):P * (qt % 4 + 1)],
                                            k_stack[:, parity, h, HALF * half:HALF * (half + 1)],
                                            start=True, stop=True)
                last.then_inc(scores_ready, 1)

            def turn_probs(fr, n, off):
                pe.wait_ge(probs_ready, fr.count(ITEMS, ITEMS * off + n + 1))
                for half, (moved, turned) in enumerate(((moved_a, turned_a), (moved_b, turned_b))):
                    wait(pe, moved, fr.count(ITEMS, ITEMS * off + n))
                    for k in range(TILES // 2):
                        last = nc.tensor.transpose(ps_turn[:, half, P * k:P * (k + 1)],
                                                   probs[:, n % RING, HALF * half + P * k:HALF * half + P * (k + 1)],
                                                   ident[:])
                    last.then_inc(turned, 1)

            def weighted_sum(fr, c, off, piece):
                g = c // CHUNKS_OF_GROUP
                if piece == 0:
                    pe.wait_ge(moved_a, fr.count(ITEMS, ITEMS * off + CHUNK * (c + 1)))
                    pe.wait_ge(moved_b, fr.count(ITEMS, ITEMS * off + CHUNK * (c + 1)))
                    wait(pe, out_moved, fr.count(CHUNKS, CHUNKS * off + c))
                if c == 0:
                    pe.wait_ge(shared_drained, fr.turn("V", PIECE * piece + PIECE - 1))
                for k in range(PIECE * piece, PIECE * (piece + 1)):
                    for h in range(GROUP):
                        col = P * g + HEAD * h
                        item = (CHUNK * c + 2 * h) % PT_RING
                        last = nc.tensor.matmul(ps_out[HEAD * h:HEAD * (h + 1), 0:PAIR_Q], values[:, k, col:col + HEAD],
                                                probs_turned[:, item:item + 2, k, :],
                                                start=(k == 0), stop=(k == TILES - 1))
                if piece == PIECES - 1:
                    last.then_inc(pv_ready, 1)

            def shared_turns(fr, n, window):
                for kind, index, off, here, pieces in fr.pieces_at(n, window):
                    if kind == "P":
                        last = project(fr, index, off, here)
                    if kind == "X":
                        last = turn_x(fr, index, off)
                    if kind == "V":
                        last = make_values(fr, index, here)
                    if kind == "O":
                        last = project_out(fr, index, off, here)
                    if pieces - 1 in here:
                        last.then_inc(shared_filled, 1)

            def frame(fr):
                for n in range(fr.slots):
                    if fr.cur:
                        scores(fr, n)
                    for piece in range(PIECES):
                        item, off = before(n, SLOT_SUM + piece)
                        if item % CHUNK == 0 and fr.has(off) and (fr.cur or off == -1) and item < ITEMS:
                            weighted_sum(fr, item // CHUNK, off, piece)
                            if piece == PIECES - 1:
                                turn_inverse(fr, item // CHUNK, off)
                    shared_turns(fr, n, 1)
                    item, off = before(n, 2)
                    if fr.has(off) and (fr.cur or off == -1):
                        turn_probs(fr, item, off)
                    shared_turns(fr, n, 2)

            pe.wait_ge(ident_loaded, 16)
            run_frames(pe, frame)

        @block.scalar
        def _(act):
            def split_hi(fr, index, off):
                j = index % 4
                group = fr.count(GROUPS, GROUPS * off + index // 4)
                act.wait_ge(shared_filled, fr.turn("P", index, off))
                wait(act, stacked[j ^ 1], (group + j % 2) * (16 * 4 * GROUP))
                if j == 2:
                    act.wait_ge(consts_loaded, fr.count(16, 16 * (off + 1)))
                scale = 1.0 if j < 2 else consts[:, (fr.odd + off) % 2, 1:2]
                nc.scalar.activation(part_hi[:, j // 2, :], ps_shared[:], ACT.Identity, scale=scale)\
                    .then_inc(hi_ready, 1)

            def move_x(fr, t, off):
                act.wait_ge(shared_filled, fr.turn("X", t, off))
                nc.scalar.activation(x_turned[:, :, P * t:P * (t + 1)],
                                     ps_shared[:, 0:HIDDEN].rearrange("p (k c) -> p k c", k=KT), ACT.Copy)\
                    .then_inc(shared_drained, 1)

            def move_inverse(fr, c, off):
                act.wait_ge(inverse_filled, fr.count(CHUNKS, CHUNKS * off + c + 1))
                nc.scalar.activation(inverse_turned[:], ps_out[:, PAIR_Q:2 * PAIR_Q], ACT.Copy).then_inc(inverse_moved, 1)

            def exponentials(fr, n):
                c = n // CHUNK
                act.wait_ge(shifted_ready, fr.count(ITEMS, n + 1))
                if n % CHUNK == 0:
                    wait(act, wide_ready, fr.count(CHUNKS, c - 1))
                col = n % CHUNK
                nc.scalar.activation(probs[:, n % RING, :], probs[:, n % RING, :], ACT.Exp,
                                     bias=neg_max[:, c % 2, col:col + 1], scale=-1.0,
                                     accum_out=row_sum[:, c % 2, col:col + 1]).then_inc(probs_ready, 1)

            def move_turned(fr, n, off):
                act.wait_ge(turned_a, fr.count(ITEMS, ITEMS * off + n + 1))
                if n % GROUP == 0:
                    wait(act, pv_ready, fr.count(CHUNKS, CHUNKS * off + (n - PT_RING) // CHUNK + 1))
                nc.scalar.activation(probs_turned[:, n % PT_RING, 0:TILES // 2, :],
                                     ps_turn[:, 0, :].rearrange("p (k q) -> p k q", q=P), ACT.Copy)\
                    .then_inc(moved_a, 1)

            def shared_turns(fr, n, window):
                for kind, index, off in fr.turns_at(n, window):
                    if kind == "P":
                        split_hi(fr, index, off)
                    if kind == "X":
                        move_x(fr, index, off)

            def frame(fr):
                for n in range(fr.slots):
                    shared_turns(fr, n, 1)
                    item, off = before(n, 2)
                    if fr.has(off) and (fr.cur or off == -1):
                        move_turned(fr, item, off)
                    if fr.cur:
                        exponentials(fr, n)
                    item, off = before(n, SLOT_NORM)
                    if item % CHUNK == 0 and fr.has(off) and (fr.cur or off == -1):
                        move_inverse(fr, item // CHUNK, off)
                    shared_turns(fr, n, 2)

            run_frames(act, frame)

        @block.vector
        def _(dve):
            def shift(fr, n):
                c = n // CHUNK
                g, h, qt = item_of(n)
                if n == 0:
                    dve.wait_ge(consts_loaded, fr.count(16, 16))
                if g == 0 and n % CHUNK == 0:
                    dve.wait_ge(adj_loaded[c], fr.count(16, 16))
                if n % CHUNK == 0:
                    wait(dve, wide_ready, fr.count(CHUNKS, c - 1))
                dve.wait_ge(scores_ready, fr.count(ITEMS, n + 1))
                wait(dve, turned_b, fr.count(ITEMS, n + 1 - RING))
                settle(dve, fr, dve_settled)
                col = n % CHUNK
                nc.vector.tensor_tensor_reduce(out=probs[:, n % RING, :], in0=ps_scores[:, n % 2, :],
                                               in1=adj_sb[:, qt, :], scale=consts[:, fr.odd, 0:1], scalar=3.0e38,
                                               op0=ALU.add, op1=ALU.min,
                                               accum_out=neg_max[:, c % 2, col:col + 1]).then_inc(shifted_ready, 1)

            def invert(fr, c, off):
                dve.wait_ge(probs_ready, fr.count(ITEMS, ITEMS * off + CHUNK * (c + 1)))
                wait(dve, wide_ready, fr.count(CHUNKS, CHUNKS * off + c - 1))
                nc.vector.reciprocal(inverse[:, c % 2, :], row_sum[:, c % 2, :]).then_inc(inverse_ready, 1)

            def split_lo(fr, index, off):
                j = index % 4
                dve.wait_ge(hi_ready, fr.count(4 * GROUPS, 4 * GROUPS * off + PROJECTED.index(index) + 1))
                hi = part_hi[:, j // 2, :].bitcast(F32)
                if j < 2:
                    ins = nc.vector.tensor_tensor(part_lo[:, j // 2, :], ps_shared[:], hi, ALU.subtract)
                else:
                    ins = nc.vector.scalar_tensor_tensor(part_lo[:, j // 2, :], ps_shared[:],
                                                         consts[:, (fr.odd + off) % 2, 1:2], hi,
                                                         ALU.mult, ALU.subtract)
                ins.then_inc(shared_drained, 1)

            def move_values(fr, t):
                if t == 0:
                    dve.wait_ge(w_odd_loaded, fr.count(64, 32))
                dve.wait_ge(shared_filled, fr.turn("V", t))
                nc.vector.tensor_tensor(values[:, t, :], ps_shared[:, 0:HIDDEN], bias_v[:], ALU.add)\
                    .then_inc(shared_drained, 1)

            def move_turned(fr, n, off):
                dve.wait_ge(turned_b, fr.count(ITEMS, ITEMS * off + n + 1))
                if n % GROUP == 0:
                    wait(dve, pv_ready, fr.count(CHUNKS, CHUNKS * off + (n - PT_RING) // CHUNK + 1))
                nc.vector.tensor_copy(probs_turned[:, n % PT_RING, TILES // 2:TILES, :],
                                      ps_turn[:, 1, :].rearrange("p (k q) -> p k q", q=P)).then_inc(moved_b, 1)

            def normalise(fr, c, off):
                g, q0 = c // CHUNKS_OF_GROUP, PAIR_Q * (c % CHUNKS_OF_GROUP)
                dve.wait_ge(pv_ready, fr.count(CHUNKS, CHUNKS * off + c + 1))
                dve.wait_ge(inverse_moved, fr.count(CHUNKS, CHUNKS * off + c + 1))
                nc.vector.tensor_tensor(out_turned[:, g, q0:q0 + PAIR_Q], ps_out[:, 0:PAIR_Q], inverse_turned[:],
                                        ALU.mult).then_inc(out_moved, 1)

            def residual(fr, t, off):
                done = fr.count(TILES, TILES * off + t + 1)
                dve.wait_ge(shared_filled, fr.turn("O", t, off))
                dve.wait_ge(res_ready, done)
                nc.vector.tensor_tensor(res[:, t % 2, :], ps_shared[:, 0:HIDDEN], res[:, t % 2, :], ALU.add)\
                    .then_inc(shared_drained, 1)

            def sum_stats(fr, t, off):
                dve.wait_ge(shared_drained, fr.turn("O", t, off))
                nc.vector.bn_stats(stats[:, t % 2, :], res[:, t % 2, :]).then_inc(stats_step, 1)

            def mean_and_variance(fr, t, off):
                dve.wait_ge(stats_step, fr.count(TILES, TILES * off + t + 1))
                settle(dve, fr, dve_settled)
                nc.vector.bn_aggr(mean_var[:, t % 2, :], stats[:, t % 2, :]).then_inc(stats_ready, 1)

            def shared_turns(fr, n, window):
                for kind, index, off in fr.turns_at(n, window):
                    if kind == "P":
                        split_lo(fr, index, off)
                    if kind == "V":
                        move_values(fr, index)
                    if kind == "O":
                        residual(fr, index, off)

            def frame(fr):
                for n in range(fr.slots):
                    if fr.cur:
                        shift(fr, n)
                    item, off = before(n, CHUNK + 1)
                    if n % CHUNK == 1 and fr.has(off) and (fr.cur or off == -1):
                        invert(fr, item // CHUNK, off)
                    shared_turns(fr, n, 1)
                    item, off = before(n, 2)
                    if fr.has(off) and (fr.cur or off == -1):
                        move_turned(fr, item, off)
                    item, off = before(n, SLOT_NORM)
                    if item % CHUNK == 0 and fr.has(off) and (fr.cur or off == -1):
                        normalise(fr, item // CHUNK, off)
                    for t in range(TILES):
                        last = TIMETABLE["O", t][-1][0]
                        for at, program in ((last + 1, sum_stats), (last + 2, mean_and_variance)):
                            if at % ITEMS == n and fr.has(-(at // ITEMS)):
                                program(fr, t, -(at // ITEMS))
                    shared_turns(fr, n, 2)

            run_frames(dve, frame)

        @block.gpsimd
        def _(pool):
            GUARD_STEPS, NORM_STEPS = 5, 3

            def widen(fr, c, off):
                base = fr.count(CHUNKS, CHUNKS * off + c) * GUARD_STEPS
                ones, keep = guard[:, 0, :], guard[:, 1, :]
                pool.wait_ge(inverse_ready, fr.count(CHUNKS, CHUNKS * off + c + 1))
                settle(pool, fr, pool_settled)
                nc.gpsimd.tensor_scalar(ones, row_sum[:, c % 2, :], float(TOKENS), -1.0, ALU.is_equal, ALU.mult)\
                    .then_inc(guard_step, 1)
                settle(pool, fr, pool_settled)
                nc.gpsimd.tensor_scalar(keep, neg_max[:, c % 2, :], 0.0, None, ALU.is_equal)\
                    .then_inc(guard_step, 1)
                pool.wait_ge(guard_step, base + 2)
                nc.gpsimd.tensor_tensor(keep, ones, keep, ALU.mult).then_inc(guard_step, 1)
                pool.wait_ge(guard_step, base + 3)
                settle(pool, fr, pool_settled)
                nc.gpsimd.tensor_scalar(ones, keep, 1.0, None, ALU.add).then_inc(guard_step, 1)
                pool.wait_ge(guard_step, base + 4)
                nc.gpsimd.tensor_tensor(keep, ones, inverse[:, c % 2, :], ALU.mult).then_inc(guard_step, 1)
                pool.wait_ge(guard_step, base + 5)
                wait(pool, inverse_filled, fr.count(CHUNKS, CHUNKS * off + c))
                settle(pool, fr, pool_settled)
                nc.gpsimd.tensor_copy(inverse_wide[:],
                                      keep.rearrange("p (h q) -> p q h", q=2).unsqueeze(3)
                                      .broadcast_to([P, 2, GROUP, HEAD])).then_inc(wide_ready, 1)

            def add_bias(fr, t, off):
                if t == 0:
                    pool.wait_ge(wo_loaded, fr.count(32, 32 * (off + 1)))
                pool.wait_ge(res_loaded[t % 2], fr.count(64, 64 * off + 16 * (t // 2 + 1)))
                nc.gpsimd.tensor_tensor(res[:, t % 2, :], res[:, t % 2, :], bias_o[:], ALU.add).then_inc(res_ready, 1)

            def layernorm(fr, t, off):
                base = fr.count(TILES, TILES * off + t) * NORM_STEPS
                pool.wait_ge(stats_ready, fr.count(TILES, TILES * off + t + 1))
                settle(pool, fr, pool_settled)
                nc.gpsimd.tensor_scalar(mean_var[:, t % 2, 1:2], mean_var[:, t % 2, 1:2], EPS, None, ALU.add)\
                    .then_inc(norm_step, 1)
                pool.wait_ge(norm_step, base + 1)
                nc.gpsimd.tensor_tensor(mean_var[:, t % 2, 1:2], mean_var[:, t % 2, 1:2], minus_half, ALU.pow)\
                    .then_inc(norm_step, 1)
                pool.wait_ge(norm_step, base + 2)
                settle(pool, fr, pool_settled)
                nc.gpsimd.tensor_scalar(res[:, t % 2, :], res[:, t % 2, :], mean_var[:, t % 2, 0:1],
                                        mean_var[:, t % 2, 1:2], ALU.subtract, ALU.mult).then_inc(norm_step, 1)
                pool.wait_ge(norm_step, base + 3)
                rows = out.rearrange("s (t p) c -> p s t c", p=P)[:, bass.ds(fr.count(1, off), 1), t, :]
                pool.dma_start(rows, res[:, t % 2:t % 2 + 1, :]).then_inc(out_stored[t % 2], 16)

            def frame(fr):
                for n in range(fr.slots):
                    item, off = before(n, CHUNK + 1)
                    if n % CHUNK == 1 and fr.has(off) and (fr.cur or off == -1):
                        widen(fr, item // CHUNK, off)
                    for t in range(TILES):
                        for at, program in ((SLOT_BIAS[t], add_bias), (TIMETABLE["O", t][-1][0] + 2, layernorm)):
                            if at % ITEMS == n and fr.has(-(at // ITEMS)):
                                program(fr, t, -(at // ITEMS))

            nc.gpsimd.memset(minus_half, -0.5).then_inc(half_set, 1)
            pool.wait_ge(half_set, 1)
            run_frames(pool, frame)
            for s in out_stored:
                pool.wait_ge(s, 16 * STEPS * TILES // 2)


def kernel(x, adj, L0_gnn_Wq, L0_gnn_Wk, L0_gnn_Wv, L0_gnn_bv, L0_gnn_Wo, L0_gnn_bo,
           L1_gnn_Wq, L1_gnn_Wk, L1_gnn_Wv, L1_gnn_bv, L1_gnn_Wo, L1_gnn_bo):
    import numpy as np
    import concourse.bacc as bacc
    from concourse.bass_utils import run_bass_kernel_spmd

    weights = np.stack([np.stack([np.asarray(w).T for w in layer]) for layer in
                        ((L0_gnn_Wq, L0_gnn_Wk, L0_gnn_Wv, L0_gnn_Wo), (L1_gnn_Wq, L1_gnn_Wk, L1_gnn_Wv, L1_gnn_Wo))])
    biases = np.stack([np.stack([np.asarray(b) for b in layer]) for layer in
                       ((L0_gnn_bv, L0_gnn_bo), (L1_gnn_bv, L1_gnn_bo))])
    layer_consts = np.array([[[-f, SCALE / f]] * P for f in (2.0, 1.0)], np.float32)
    arrays = {"x": np.asarray(x), "adj": np.asarray(adj), "weights": np.ascontiguousarray(weights),
              "biases": np.ascontiguousarray(biases), "layer_consts": layer_consts,
              "identity": np.eye(P, dtype=np.float32)}
    nc = bacc.Bacc("TRN2", target_bir_lowering=False, num_devices=1)
    args = [nc.dram_tensor(f"in_{n}", a.shape, mybir.dt.from_np(a.dtype), kind="ExternalInput").ap()
            for n, a in arrays.items()]
    out = nc.dram_tensor("out", (STEPS, TOKENS, HIDDEN), F32, kind="ExternalOutput").ap()
    build(nc, *args, out)
    r = run_bass_kernel_spmd(nc, [{f"in_{n}": a for n, a in arrays.items()}], core_ids=[0])
    return r.results[0]["out"][BATCH:]
```

```python
from contextlib import ExitStack

import concourse.bass as bass
from concourse import mybir

P = 128
LAYERS, BATCH, TOKENS, HIDDEN, HEADS = 2, 8, 1024, 384, 12
HEAD = HIDDEN // HEADS
STEPS = LAYERS * BATCH
KT = HIDDEN // P
TILES = TOKENS // P
GROUP = P // HEAD
GROUPS = HEADS // GROUP
HALF = TOKENS // 2
CHUNK = 2 * GROUP
CHUNKS = GROUPS * TILES // 2
CHUNKS_OF_GROUP = CHUNKS // GROUPS
ITEMS = CHUNKS * CHUNK
ITEMS_OF_GROUP = ITEMS // GROUPS
PAIR_Q = 2 * P
RING = 3
EPS = 1e-5
SCALE = float(HIDDEN) ** -0.5

F32 = mybir.dt.float32
F32R = mybir.dt.float32r
ACT = mybir.ActivationFunctionType
ALU = mybir.AluOpType

PT_RING = 12
PIECES = 4
PIECE = TILES // PIECES
SLOT_SUM = CHUNK + 3
SLOT_INVERSE = SLOT_SUM + PIECES - 1
SLOT_NORM = SLOT_INVERSE + 1

TIMETABLE = {("V", t): [(5 + t, 2)] * 3 for t in range(TILES)}
TIMETABLE |= {("X", t): [(slot - ITEMS, 1)] for t, slot in enumerate((45, 46, 50, 51, 58, 59, 62, 63))}
TIMETABLE |= {("O", t): at for t, at in enumerate((
    [(80, 2), (81, 1), (81, 1)], [(82, 2), (83, 1), (83, 2)], [(89, 2), (90, 1), (90, 2)],
    [(95, 1), (95, 2), (95, 2)], [(111, 2), (112, 1), (112, 2)], [(121, 1), (121, 2), (122, 1)],
    [(123, 1), (123, 2), (124, 1)], [(129, 2), (130, 1), (130, 2)]))}
TIMETABLE |= {("P", n): at for n, at in enumerate((
    [(64 - ITEMS, 1), (65 - ITEMS, 1), (66 - ITEMS, 1)], [(73 - ITEMS, 1), (74 - ITEMS, 1), (79 - ITEMS, 1)],
    [(71 - ITEMS, 1), (71 - ITEMS, 2), (72 - ITEMS, 1)], [(87 - ITEMS, 1), (87 - ITEMS, 2), (88 - ITEMS, 1)],
    [(0, 2), (1, 1), (2, 1)], [(17, 2), (18, 1), (19, 1)],
    [(23, 1), (23, 2), (24, 1)], [(31, 1), (31, 2), (32, 1)],
    [(39, 1), (39, 2), (40, 1)], [(47, 1), (48, 1), (49, 1)],
    [(41, 1), (41, 2), (42, 1)], [(55, 1), (56, 1), (57, 1)]))}
PROJECTED = sorted(range(4 * GROUPS), key=lambda n: TIMETABLE["P", n])
SLOT_STACK = [-28, -12, -16, 0, 3, 20, 25, 33, 41, 52, 48, 64]
HEAD_STACK = 2
SLOT_RES = [74, 76, 86, 88, 105, 113, 117, 127]
SLOT_BIAS = [77, 78, 88, 93, 108, 116, 120, 129]
SLOT_X = [38, 38, 47, 47, 52, 52, 60, 60]
SLOT_W_V, SLOT_W_QK = 59 - ITEMS, [43 - ITEMS, 91 - ITEMS, 14]
TAIL_TILES = (4, 5)
TAIL = 38


def turns_of_frame():
    turns = []
    for (kind, index), pieces in TIMETABLE.items():
        off = -(pieces[0][0] // ITEMS)
        assert pieces[-1][0] // ITEMS == -off
        turns.append(([(slot + ITEMS * off, window) for slot, window in pieces], kind, index, off))
    turns.sort()
    assert all(a[0][-1] <= b[0][0] for a, b in zip(turns, turns[1:]))
    return turns


TURNS = turns_of_frame()
assert all(pieces[-1][1] == 1 for pieces, kind, index, off in TURNS if kind == "P")
BEFORE = sum(1 for t in TURNS if t[3] == 1) - sum(1 for t in TURNS if t[3] == -1)


class Frame:

    def __init__(self, pair, odd, first=0, last=0):
        self.pair, self.odd = pair, odd
        self.f = 2 * pair + odd if isinstance(pair, int) else None
        f = self.f
        self.prev = f is None or f > 0
        self.cur = f is None or 0 <= f < STEPS
        self.next = f is None or f < STEPS - 1
        self.slots = ITEMS if f is None or f < STEPS else TAIL

    def count(self, per_step, n):
        return self.pair * (2 * per_step) + (self.odd * per_step + n)

    def has(self, off):
        return (self.prev, self.cur, self.next)[off + 1]

    def turn(self, kind, index, off=0):
        at = next(n for n, t in enumerate(TURNS) if t[1] == kind and t[2] == index)
        frame_off = off - TURNS[at][3]
        if self.f is None:
            return self.count(len(TURNS), frame_off * len(TURNS) + BEFORE + at + 1)
        return sum(1 for f in range(-1, self.f + frame_off + 1)
                   for t in (TURNS if f < self.f + frame_off else TURNS[:at + 1]) if 0 <= f + t[3] < STEPS)

    def projection(self, index, off):
        return self.count(4 * GROUPS, 4 * GROUPS * off + PROJECTED.index(index) + 1)

    def pieces_at(self, slot, window):
        found = []
        for pieces, kind, index, off in TURNS:
            here = [n for n, at in enumerate(pieces) if at == (slot, window)]
            if here and self.has(off):
                found.append((kind, index, off, here, len(pieces)))
        return found

    def turns_at(self, slot, window):
        return [(k, i, off) for k, i, off, here, n in self.pieces_at(slot, window) if n - 1 in here]


STACK_LAG = (ITEMS_OF_GROUP, ITEMS_OF_GROUP, ITEMS_OF_GROUP // 2, 0)
assert all(slot >= max(TIMETABLE["P", n][-1][0] + 1, ITEMS_OF_GROUP * (n // 4) - STACK_LAG[n % 4])
           for n, slot in enumerate(SLOT_STACK))


def wait(eng, sem, value):
    if not (isinstance(value, int) and value <= 0):
        eng.wait_ge(sem, value)


def settle(eng, fr, counter):
    if fr.f is None:
        eng.sem_inc(counter, 1)


def run_frames(eng, frame_program):
    frame_program(Frame(-1, 1))
    frame_program(Frame(0, 0))
    frame_program(Frame(0, 1))
    with eng.Fori(1, STEPS // 2 - 1) as pair:
        frame_program(Frame(pair, 0))
        frame_program(Frame(pair, 1))
    frame_program(Frame(STEPS // 2 - 1, 0))
    frame_program(Frame(STEPS // 2 - 1, 1))
    frame_program(Frame(STEPS // 2, 0))


def item_of(n):
    chunk = n // CHUNK
    return chunk // CHUNKS_OF_GROUP, (n % CHUNK) // 2, 2 * (chunk % CHUNKS_OF_GROUP) + n % 2


def before(n, lag):
    return (n - lag, 0) if n >= lag else (n - lag + ITEMS, -1)


def build(nc, x, adj, weights, biases, layer_consts, identity, out):
    ctx = ExitStack()
    with ctx:
        def sb(name, shape, dt=F32):
            return ctx.enter_context(nc.sbuf_tensor(name, shape, dt))

        def psum(name, shape):
            return ctx.enter_context(nc.psum_tensor(name, shape, F32))

        def sem(name):
            return ctx.enter_context(nc.semaphore(name))

        ident = sb("ident", [P, P])
        x_in = sb("x_in", [P, 2, HIDDEN])
        x_turned = sb("x_turned", [P, KT, TOKENS])
        w_even = sb("w_even", [P, 2, KT, P])
        w_odd = sb("w_odd", [P, KT * HIDDEN])
        w_v = w_odd[:].rearrange("p (k c) -> p k c", k=KT)
        w_qk = (w_even[:], w_even[:], w_odd[:, 0:2 * KT * P].rearrange("p (w k c) -> p w k c", w=2, k=KT))
        w_o = sb("w_o", [P, KT, HIDDEN])
        bias_v = sb("bias_v", [P, HIDDEN])
        bias_o = sb("bias_o", [P, HIDDEN])
        factors = sb("factors", [P, 5])
        consts = factors[:, 0:4].rearrange("p (b i) -> p b i", b=2)
        minus_half = factors[:, 4:5]
        part_hi = sb("part_hi", [P, 2, HALF], F32R)
        part_lo = sb("part_lo", [P, 2, HALF])
        k_stack = sb("k_stack", [P, 2, GROUP, TOKENS], F32R)
        q_stack = sb("q_stack", [P, 2, GROUP, HALF], F32R)
        adj_sb = sb("adj_sb", [P, TILES, TOKENS])
        probs = sb("probs", [P, RING, TOKENS])
        neg_max = sb("neg_max", [P, 2, CHUNK])
        row_sum = sb("row_sum", [P, 2, CHUNK])
        inverse = sb("inverse", [P, 2, CHUNK])
        guard = sb("guard", [P, 2, CHUNK])
        inverse_wide = sb("inverse_wide", [P, 2, GROUP, HEAD])
        inverse_turned = sb("inverse_turned", [P, PAIR_Q])
        probs_turned = sb("probs_turned", [P, PT_RING, TILES, P])
        values = sb("values", [P, TILES, HIDDEN])
        out_turned = sb("out_turned", [P, GROUPS, TOKENS])
        res = sb("res", [P, 2, HIDDEN])
        layer_stats = sb("layer_stats", [P, 2, 8])
        stats = layer_stats[:, :, 0:6]
        mean_var = layer_stats[:, :, 6:8]

        ps_scores = psum("ps_scores", [P, 2, TOKENS])
        ps_turn = psum("ps_turn", [P, 2, HALF])
        ps_out = psum("ps_out", [P, HALF])
        ps_shared = psum("ps_shared", [P, HALF])

        ident_loaded = sem("ident_loaded")
        x_loaded = [sem(f"x_loaded{i}") for i in range(2)]
        w_even_loaded, w_odd_loaded = sem("w_even_loaded"), sem("w_odd_loaded")
        wo_loaded = sem("wo_loaded")
        consts_loaded = sem("consts_loaded")
        stacked = [sem(f"stacked_{n}") for n in ("k0", "k1", "q0", "q1")]
        stacked_in_head = sem("stacked_in_head")
        adj_loaded = [sem(f"adj_loaded{j}") for j in range(TILES // 2)]
        res_loaded = [sem(f"res_loaded{i}") for i in range(2)]
        shared_filled = sem("shared_filled")
        shared_drained = sem("shared_drained")
        hi_ready = sem("hi_ready")
        lo_ready = sem("lo_ready")
        scores_ready = sem("scores_ready")
        shifted_ready = sem("shifted_ready")
        probs_ready = sem("probs_ready")
        turned_a = sem("turned_a")
        turned_b = sem("turned_b")
        moved_a = sem("moved_a")
        moved_b = sem("moved_b")
        pv_ready = sem("pv_ready")
        out_moved = sem("out_moved")
        inverse_filled = sem("inverse_filled")
        inverse_moved = sem("inverse_moved")
        inverse_ready = sem("inverse_ready")
        guard_step = sem("guard_step")
        wide_ready = sem("wide_ready")
        res_ready = sem("res_ready")
        stats_step = sem("stats_step")
        stats_ready = sem("stats_ready")
        eps_added = sem("eps_added")
        deviation_ready = sem("deviation_ready")
        normed = sem("normed")
        half_set = sem("half_set")
        tail_stored = [sem(f"tail_stored{i}") for i in range(2)]
        out_stored = [sem(f"out_stored{i}") for i in range(2)]

        sp_settled, dve_settled, pool_settled = sem("sp_settled"), sem("dve_settled"), sem("pool_settled")

        def tile_of(fr, t):
            return x_in if fr.f == STEPS and t in TAIL_TILES else res

        def loaded(fr, t, off):
            if tile_of(fr, t) is x_in:
                return x_loaded[t % 2], 16 * (STEPS * TILES // 2 + 1)
            fewer = 1 if fr.f == STEPS and t > TAIL_TILES[1] else 0
            return res_loaded[t % 2], fr.count(64, 64 * off + 16 * (t // 2 + 1 - fewer))

        block = ctx.enter_context(nc.Block())

        def stack_dmas(eng, eng_settled, stacked, fr, index, off):
            g, j = divmod(index, 4)
            buf = j // 2
            wait(eng, lo_ready, fr.projection(index, off))
            settle(eng, fr, eng_settled)
            wait(eng, scores_ready, fr.count(ITEMS, ITEMS * off + ITEMS_OF_GROUP * g - STACK_LAG[j]))
            settle(eng, fr, eng_settled)
            for block_row in range(4):
                low = block_row % 2 if j >= 2 else block_row // 2
                part = part_lo[:] if low else part_hi[:].bitcast(F32)
                rows = slice(HEAD * block_row, HEAD * (block_row + 1))
                for h in range(GROUP):
                    src = part[HEAD * h:HEAD * (h + 1), buf, :]
                    if j < 2:
                        parity = (GROUPS * (fr.odd + off) + g) % 2
                        dst = k_stack[rows, parity, h, HALF * j:HALF * (j + 1)]
                    else:
                        dst = q_stack[rows, j - 2, h, :]
                    eng.dma_start(dst.bitcast(F32), src).then_inc(stacked[j], 16)

        def split_lo(eng, fr, index, off):
            buf = index % 4 // 2
            eng.wait_ge(hi_ready, fr.projection(index, off))
            eng.tensor_tensor(part_lo[:, buf, :], part_lo[:, buf, :], part_hi[:, buf, :].bitcast(F32),
                              ALU.subtract).then_inc(lo_ready, 1)

        @block.sync
        def _(sp):
            def sp_wait(fr, sem, value):
                wait(sp, sem, value)
                settle(sp, fr, sp_settled)

            def frame(fr, layer, next_layer):
                def rows(tensor, off, in_layer, t0, n, cols):
                    b = fr.count(1, off - BATCH * in_layer)
                    view = tensor.rearrange("b (t p) c -> p b t c", p=P)
                    return view[:, bass.ds(b, 1), t0:t0 + n, :].rearrange("p b t c -> p (b t) c")

                def x_rows(off, in_layer, t):
                    return rows(out if in_layer else x, off, in_layer, t, 1, HIDDEN)

                def stored_before(off, in_layer):
                    if in_layer:
                        for s in out_stored:
                            sp_wait(fr, s, fr.count(64, 64 * (off - BATCH + 1)))

                for n in range(fr.slots):
                    if fr.cur and n == TAIL - 2:
                        if fr.prev:
                            sp_wait(fr, shared_filled, fr.turn("O", TILES - 1, -1))
                        sp_wait(fr, res_ready, fr.count(TILES, 0))
                        sp.dma_start(w_o[:], weights[layer, 3].rearrange("(k p) o -> p k o", p=P))\
                            .then_inc(wo_loaded, 16)
                        sp.dma_start(bias_o[:], biases[layer, 1].partition_broadcast(P)).then_inc(wo_loaded, 16)
                    if fr.next and n == SLOT_W_V + ITEMS:
                        if fr.cur:
                            sp_wait(fr, shared_filled, fr.turn("P", PROJECTED[-1]))
                        sp.dma_start(w_v, weights[next_layer, 2].rearrange("(k p) o -> p k o", p=P))\
                            .then_inc(w_odd_loaded, 16)
                        sp.dma_start(bias_v[:], biases[next_layer, 0].partition_broadcast(P))\
                            .then_inc(w_odd_loaded, 16)
                    for g, slot in enumerate(SLOT_W_QK):
                        off = -(slot // ITEMS)
                        if n == slot % ITEMS and fr.has(off):
                            if g == 2:
                                sp_wait(fr, shared_filled, fr.turn("V", TILES - 1))
                            elif g == 1:
                                sp_wait(fr, shared_filled, fr.turn("P", 3, 1))
                            elif fr.cur:
                                sp_wait(fr, shared_filled, fr.turn("P", 7))
                            for w in range(2):
                                src = weights[next_layer if off else layer, w].rearrange("(k p) o -> p k o", p=P)
                                sp.dma_start(w_qk[g][:, w], src[:, :, P * g:P * (g + 1)])\
                                    .then_inc(w_odd_loaded if g == 2 else w_even_loaded, 16)
                    if fr.next and n == 12:
                        sp_wait(fr, shifted_ready, fr.count(ITEMS, 0))
                        sp.dma_start(consts[:, 1 - fr.odd, :], layer_consts[next_layer]).then_inc(consts_loaded, 16)
                    for t in range(TILES):
                        if fr.next and n == SLOT_X[t]:
                            if t == 0:
                                stored_before(1, next_layer)
                            if t >= 2:
                                sp_wait(fr, shared_filled, fr.turn("X", t - 2, 1))
                            elif fr.cur:
                                sp_wait(fr, shared_filled, fr.turn("X", TILES - 2 + t, 0))
                            sp.dma_start(x_in[:, t % 2:t % 2 + 1, :], x_rows(1, next_layer, t))\
                                .then_inc(x_loaded[t % 2], 16)
                    for t, slot in enumerate(SLOT_RES):
                        off = -(slot // ITEMS)
                        if slot % ITEMS == n and fr.has(off):
                            if t == 0:
                                stored_before(off, layer)
                            lag = 2 if fr.f == STEPS and t >= TAIL_TILES[0] else 1
                            sp_wait(fr, out_stored[t % 2], fr.count(64, 64 * off + 16 * (t // 2 + 1 - lag)))
                            in_layer = layer if off == 0 or fr.f != BATCH else 0
                            sp.dma_start(tile_of(fr, t)[:, t % 2:t % 2 + 1, :], x_rows(off, in_layer, t)).then_inc(loaded(fr, t, off)[0], 16)
                    for index, slot in enumerate(SLOT_STACK):
                        off = -(slot // ITEMS)
                        if slot % ITEMS == n and fr.has(off) and (index != HEAD_STACK or fr.f != -1):
                            stack_dmas(sp, sp_settled, stacked, fr, index, off)
                    j = (n - 2 * ITEMS_OF_GROUP - CHUNK - 1) // CHUNK if n > ITEMS_OF_GROUP else -1
                    if n % CHUNK == 1 and (0 <= j < 3 and fr.next or n == 1 and fr.cur):
                        off = 1
                        if n == 1:
                            j, off = 3, 0
                        sp_wait(fr, shifted_ready, fr.count(ITEMS, ITEMS * off - ITEMS_OF_GROUP + CHUNK * (j + 1)))
                        in_layer = next_layer if off else layer
                        sp.dma_start(adj_sb[:, 2 * j:2 * j + 2, :], rows(adj, off, in_layer, 2 * j, 2, TOKENS))\
                            .then_inc(adj_loaded[j], 16)

            sp.dma_start(ident[:], identity).then_inc(ident_loaded, 16)
            frame(Frame(-1, 1), 0, 0)
            mid = BATCH // 2
            frame(Frame(0, 0), 0, 0)
            frame(Frame(0, 1), 0, 0)
            with sp.Fori(1, mid - 1) as pair:
                frame(Frame(pair, 0), 0, 0)
                frame(Frame(pair, 1), 0, 0)
            frame(Frame(mid - 1, 0), 0, 0)
            frame(Frame(mid - 1, 1), 0, 1)
            frame(Frame(mid, 0), 1, 1)
            frame(Frame(mid, 1), 1, 1)
            with sp.Fori(mid + 1, STEPS // 2 - 1) as pair:
                frame(Frame(pair, 0), 1, 1)
                frame(Frame(pair, 1), 1, 1)
            frame(Frame(STEPS // 2 - 1, 0), 1, 1)
            frame(Frame(STEPS // 2 - 1, 1), 1, 1)
            frame(Frame(STEPS // 2, 0), 1, 1)

        @block.tensor
        def _(pe):
            def project(fr, index, off, here):
                g, j = divmod(index, 4)
                is_key = j < 2
                if 0 in here:
                    if j == 0:
                        pe.wait_ge((w_even_loaded, w_even_loaded, w_odd_loaded)[g],
                                   fr.count(64, 64 * off + (32, 64, 64)[g]))
                    wait(pe, shared_drained, fr.turn("P", index, off) - 1)
                for k in here:
                    last = nc.tensor.matmul(ps_shared[:], w_qk[g][:, int(is_key), k, :],
                                            x_turned[:, k, HALF * (j % 2):HALF * (j % 2 + 1)],
                                            start=(k == 0), stop=(k == KT - 1))
                return last

            def turn_x(fr, t, off):
                pe.wait_ge(x_loaded[t % 2], fr.count(64, 64 * off + 16 * (t // 2 + 1)))
                wait(pe, shared_drained, fr.turn("X", t, off) - 1)
                for k in range(KT):
                    last = nc.tensor.transpose(ps_shared[:, P * k:P * (k + 1)], x_in[:, t % 2, P * k:P * (k + 1)],
                                               ident[:])
                return last

            def make_values(fr, t, here):
                if 0 in here:
                    if t == 0:
                        pe.wait_ge(w_odd_loaded, fr.count(64, 32))
                    wait(pe, shared_drained, fr.turn("V", t) - 1)
                for k in here:
                    last = nc.tensor.matmul(ps_shared[:, 0:HIDDEN], x_turned[:, k, P * t:P * (t + 1)], w_v[:, k, :],
                                            start=(k == 0), stop=(k == KT - 1))
                return last

            def project_out(fr, t, off, here):
                if 0 in here:
                    if t == 0:
                        pe.wait_ge(wo_loaded, fr.count(32, 32 * (off + 1)))
                    pe.wait_ge(out_moved, fr.count(CHUNKS, CHUNKS * off + 2 * CHUNKS_OF_GROUP + t // 2 + 1))
                    wait(pe, shared_drained, fr.turn("O", t, off) - 1)
                for k in here:
                    last = nc.tensor.matmul(ps_shared[:, 0:HIDDEN], out_turned[:, k, P * t:P * (t + 1)], w_o[:, k, :],
                                            start=(k == 0), stop=(k == GROUPS - 1))
                return last

            def turn_inverse(fr, c, off):
                pe.wait_ge(wide_ready, fr.count(CHUNKS, CHUNKS * off + c + 1))
                for q in range(2):
                    last = nc.tensor.transpose(ps_out[:, PAIR_Q + P * q:PAIR_Q + P * (q + 1)],
                                               inverse_wide[:, q].rearrange("p h d -> p (h d)"), ident[:])
                last.then_inc(inverse_filled, 1)

            def scores(fr, n):
                g, h, qt = item_of(n)
                group = fr.count(GROUPS, g + 1)
                if n % ITEMS_OF_GROUP == 0:
                    for s in stacked[0:3]:
                        pe.wait_ge(s, group * (16 * 4 * GROUP))
                if n % ITEMS_OF_GROUP == ITEMS_OF_GROUP // 2:
                    pe.wait_ge(stacked[3], group * (16 * 4 * GROUP))
                wait(pe, shifted_ready, fr.count(ITEMS, n - 1))
                parity = (GROUPS * fr.odd + g) % 2
                for half in range(2):
                    last = nc.tensor.matmul(ps_scores[:, n % 2, HALF * half:HALF * (half + 1)],
                                            q_stack[:, qt // 4, h, P * (qt % 4):P * (qt % 4 + 1)],
                                            k_stack[:, parity, h, HALF * half:HALF * (half + 1)],
                                            start=True, stop=True)
                last.then_inc(scores_ready, 1)

            def turn_probs(fr, n, off):
                pe.wait_ge(probs_ready, fr.count(ITEMS, ITEMS * off + n + 1))
                for half, (moved, turned) in enumerate(((moved_a, turned_a), (moved_b, turned_b))):
                    wait(pe, moved, fr.count(ITEMS, ITEMS * off + n))
                    for k in range(TILES // 2):
                        last = nc.tensor.transpose(ps_turn[:, half, P * k:P * (k + 1)],
                                                   probs[:, n % RING, HALF * half + P * k:HALF * half + P * (k + 1)],
                                                   ident[:])
                    last.then_inc(turned, 1)

            def weighted_sum(fr, c, off, piece):
                g = c // CHUNKS_OF_GROUP
                if piece == 0:
                    pe.wait_ge(moved_a, fr.count(ITEMS, ITEMS * off + CHUNK * (c + 1)))
                    pe.wait_ge(moved_b, fr.count(ITEMS, ITEMS * off + CHUNK * (c + 1)))
                    wait(pe, out_moved, fr.count(CHUNKS, CHUNKS * off + c))
                if c == 0:
                    pe.wait_ge(shared_drained, fr.turn("V", PIECE * piece + PIECE - 1))
                for k in range(PIECE * piece, PIECE * (piece + 1)):
                    for h in range(GROUP):
                        col = P * g + HEAD * h
                        item = (CHUNK * c + 2 * h) % PT_RING
                        last = nc.tensor.matmul(ps_out[HEAD * h:HEAD * (h + 1), 0:PAIR_Q], values[:, k, col:col + HEAD],
                                                probs_turned[:, item:item + 2, k, :],
                                                start=(k == 0), stop=(k == TILES - 1))
                if piece == PIECES - 1:
                    last.then_inc(pv_ready, 1)

            def shared_turns(fr, n, window):
                for kind, index, off, here, pieces in fr.pieces_at(n, window):
                    if kind == "P":
                        last = project(fr, index, off, here)
                    if kind == "X":
                        last = turn_x(fr, index, off)
                    if kind == "V":
                        last = make_values(fr, index, here)
                    if kind == "O":
                        last = project_out(fr, index, off, here)
                    if pieces - 1 in here:
                        last.then_inc(shared_filled, 1)

            def frame(fr):
                for n in range(fr.slots):
                    if fr.cur:
                        scores(fr, n)
                    for piece in range(PIECES):
                        item, off = before(n, SLOT_SUM + piece)
                        if item % CHUNK == 0 and fr.has(off) and (fr.cur or off == -1) and item < ITEMS:
                            weighted_sum(fr, item // CHUNK, off, piece)
                            if piece == PIECES - 1:
                                turn_inverse(fr, item // CHUNK, off)
                    shared_turns(fr, n, 1)
                    item, off = before(n, 2)
                    if fr.has(off) and (fr.cur or off == -1):
                        turn_probs(fr, item, off)
                    shared_turns(fr, n, 2)

            pe.wait_ge(ident_loaded, 16)
            run_frames(pe, frame)

        @block.scalar
        def _(act):
            def move_projected(fr, index, off):
                j = index % 4
                group = fr.count(GROUPS, GROUPS * off + index // 4)
                act.wait_ge(shared_filled, fr.turn("P", index, off))
                wait(act, stacked[j ^ 1], (group + j % 2) * (16 * 4 * GROUP))
                if j == 2:
                    act.wait_ge(consts_loaded, fr.count(16, 16 * (off + 1)))
                scale = 1.0 if j < 2 else consts[:, (fr.odd + off) % 2, 1:2]
                nc.scalar.activation(part_lo[:, j // 2, :], ps_shared[:], ACT.Identity, scale=scale)\
                    .then_inc(shared_drained, 1)

            def split_hi(fr, index, off):
                buf = index % 4 // 2
                act.wait_ge(shared_drained, fr.turn("P", index, off))
                nc.scalar.activation(part_hi[:, buf, :], part_lo[:, buf, :], ACT.Copy).then_inc(hi_ready, 1)

            def move_x(fr, t, off):
                act.wait_ge(shared_filled, fr.turn("X", t, off))
                nc.scalar.activation(x_turned[:, :, P * t:P * (t + 1)],
                                     ps_shared[:, 0:HIDDEN].rearrange("p (k c) -> p k c", k=KT), ACT.Copy)\
                    .then_inc(shared_drained, 1)

            def move_inverse(fr, c, off):
                act.wait_ge(inverse_filled, fr.count(CHUNKS, CHUNKS * off + c + 1))
                nc.scalar.activation(inverse_turned[:], ps_out[:, PAIR_Q:2 * PAIR_Q], ACT.Copy).then_inc(inverse_moved, 1)

            def exponentials(fr, n):
                c = n // CHUNK
                act.wait_ge(shifted_ready, fr.count(ITEMS, n + 1))
                if n % CHUNK == 0:
                    wait(act, wide_ready, fr.count(CHUNKS, c - 1))
                col = n % CHUNK
                nc.scalar.activation(probs[:, n % RING, :], probs[:, n % RING, :], ACT.Exp,
                                     bias=neg_max[:, c % 2, col:col + 1], scale=-1.0,
                                     accum_out=row_sum[:, c % 2, col:col + 1]).then_inc(probs_ready, 1)

            def move_turned(fr, n, off):
                act.wait_ge(turned_a, fr.count(ITEMS, ITEMS * off + n + 1))
                if n % GROUP == 0:
                    wait(act, pv_ready, fr.count(CHUNKS, CHUNKS * off + (n - PT_RING) // CHUNK + 1))
                nc.scalar.activation(probs_turned[:, n % PT_RING, 0:TILES // 2, :],
                                     ps_turn[:, 0, :].rearrange("p (k q) -> p k q", q=P), ACT.Copy)\
                    .then_inc(moved_a, 1)

            def shared_turns(fr, n, window):
                for kind, index, off in fr.turns_at(n, window):
                    if kind == "P":
                        move_projected(fr, index, off)
                    if kind == "X":
                        move_x(fr, index, off)

            def frame(fr):
                for n in range(fr.slots):
                    shared_turns(fr, n, 1)
                    item, off = before(n, 2)
                    if fr.has(off) and (fr.cur or off == -1):
                        move_turned(fr, item, off)
                    if fr.cur:
                        exponentials(fr, n)
                    item, off = before(n, SLOT_INVERSE)
                    if item % CHUNK == 0 and fr.has(off) and (fr.cur or off == -1):
                        move_inverse(fr, item // CHUNK, off)
                    for kind, index, off in fr.turns_at(n, 1):
                        if kind == "P":
                            split_hi(fr, index, off)
                    shared_turns(fr, n, 2)

            run_frames(act, frame)

        @block.vector
        def _(dve):
            def shift(fr, n):
                c = n // CHUNK
                g, h, qt = item_of(n)
                if n == 0:
                    dve.wait_ge(consts_loaded, fr.count(16, 16))
                if g == 0 and n % CHUNK == 0:
                    dve.wait_ge(adj_loaded[c], fr.count(16, 16))
                if n % CHUNK == 0:
                    wait(dve, wide_ready, fr.count(CHUNKS, c - 1))
                dve.wait_ge(scores_ready, fr.count(ITEMS, n + 1))
                wait(dve, turned_b, fr.count(ITEMS, n + 1 - RING))
                settle(dve, fr, dve_settled)
                col = n % CHUNK
                nc.vector.tensor_tensor_reduce(out=probs[:, n % RING, :], in0=ps_scores[:, n % 2, :],
                                               in1=adj_sb[:, qt, :], scale=consts[:, fr.odd, 0:1], scalar=3.0e38,
                                               op0=ALU.add, op1=ALU.min,
                                               accum_out=neg_max[:, c % 2, col:col + 1]).then_inc(shifted_ready, 1)

            def invert(fr, c, off):
                dve.wait_ge(probs_ready, fr.count(ITEMS, ITEMS * off + CHUNK * (c + 1)))
                wait(dve, wide_ready, fr.count(CHUNKS, CHUNKS * off + c - 1))
                nc.vector.reciprocal(inverse[:, c % 2, :], row_sum[:, c % 2, :]).then_inc(inverse_ready, 1)

            def move_values(fr, t):
                if t == 0:
                    dve.wait_ge(w_odd_loaded, fr.count(64, 32))
                dve.wait_ge(shared_filled, fr.turn("V", t))
                nc.vector.tensor_tensor(values[:, t, :], ps_shared[:, 0:HIDDEN], bias_v[:], ALU.add)\
                    .then_inc(shared_drained, 1)

            def move_turned(fr, n, off):
                dve.wait_ge(turned_b, fr.count(ITEMS, ITEMS * off + n + 1))
                if n % GROUP == 0:
                    wait(dve, pv_ready, fr.count(CHUNKS, CHUNKS * off + (n - PT_RING) // CHUNK + 1))
                nc.vector.tensor_copy(probs_turned[:, n % PT_RING, TILES // 2:TILES, :],
                                      ps_turn[:, 1, :].rearrange("p (k q) -> p k q", q=P)).then_inc(moved_b, 1)

            def normalise(fr, c, off):
                g, q0 = c // CHUNKS_OF_GROUP, PAIR_Q * (c % CHUNKS_OF_GROUP)
                dve.wait_ge(pv_ready, fr.count(CHUNKS, CHUNKS * off + c + 1))
                dve.wait_ge(inverse_moved, fr.count(CHUNKS, CHUNKS * off + c + 1))
                nc.vector.tensor_tensor(out_turned[:, g, q0:q0 + PAIR_Q], ps_out[:, 0:PAIR_Q], inverse_turned[:],
                                        ALU.mult).then_inc(out_moved, 1)

            def residual(fr, t, off):
                done = fr.count(TILES, TILES * off + t + 1)
                dve.wait_ge(shared_filled, fr.turn("O", t, off))
                dve.wait_ge(res_ready, done)
                nc.vector.tensor_tensor(tile_of(fr, t)[:, t % 2, :], ps_shared[:, 0:HIDDEN], tile_of(fr, t)[:, t % 2, :], ALU.add)\
                    .then_inc(shared_drained, 1)

            def mean_and_variance(fr, t, off):
                dve.wait_ge(shared_drained, fr.turn("O", t, off))
                nc.vector.bn_stats(stats[:, t % 2, :], tile_of(fr, t)[:, t % 2, :]).then_inc(stats_step, 1)
                dve.wait_ge(stats_step, fr.count(TILES, TILES * off + t + 1))
                settle(dve, fr, dve_settled)
                nc.vector.bn_aggr(mean_var[:, t % 2, :], stats[:, t % 2, :]).then_inc(stats_ready, 1)

            def layernorm(fr, t, off):
                dve.wait_ge(deviation_ready, fr.count(TILES, TILES * off + t + 1))
                settle(dve, fr, dve_settled)
                nc.vector.tensor_scalar(tile_of(fr, t)[:, t % 2, :], tile_of(fr, t)[:, t % 2, :], mean_var[:, t % 2, 0:1],
                                        mean_var[:, t % 2, 1:2], ALU.subtract, ALU.mult).then_inc(normed, 1)

            def shared_turns(fr, n, window):
                for kind, index, off in fr.turns_at(n, window):
                    if kind == "V":
                        move_values(fr, index)
                    if kind == "O":
                        residual(fr, index, off)

            def frame(fr):
                for n in range(fr.slots):
                    if fr.cur:
                        shift(fr, n)
                    item, off = before(n, CHUNK + 1)
                    if n % CHUNK == 1 and fr.has(off) and (fr.cur or off == -1):
                        invert(fr, item // CHUNK, off)
                    if fr.f == -1:
                        for kind, index, off in fr.turns_at(n, 1):
                            if kind == "P":
                                split_lo(dve, fr, index, off)
                    item, off = before(n, SLOT_NORM)
                    if item % CHUNK == 0 and fr.has(off) and (fr.cur or off == -1):
                        normalise(fr, item // CHUNK, off)
                    shared_turns(fr, n, 1)
                    item, off = before(n, 2)
                    if fr.has(off) and (fr.cur or off == -1):
                        move_turned(fr, item, off)
                    for t in range(TILES):
                        last = TIMETABLE["O", t][-1][0]
                        for at, program in ((last + 2, mean_and_variance), (last + 3, layernorm)):
                            if at % ITEMS == n and fr.has(-(at // ITEMS)):
                                program(fr, t, -(at // ITEMS))
                    shared_turns(fr, n, 2)

            run_frames(dve, frame)

        @block.gpsimd
        def _(pool):
            GUARD_STEPS = 5

            def widen(fr, c, off):
                base = fr.count(CHUNKS, CHUNKS * off + c) * GUARD_STEPS
                ones, keep = guard[:, 0, :], guard[:, 1, :]
                pool.wait_ge(inverse_ready, fr.count(CHUNKS, CHUNKS * off + c + 1))
                settle(pool, fr, pool_settled)
                nc.gpsimd.tensor_scalar(ones, row_sum[:, c % 2, :], float(TOKENS), -1.0, ALU.is_equal, ALU.mult)\
                    .then_inc(guard_step, 1)
                settle(pool, fr, pool_settled)
                nc.gpsimd.tensor_scalar(keep, neg_max[:, c % 2, :], 0.0, None, ALU.is_equal)\
                    .then_inc(guard_step, 1)
                pool.wait_ge(guard_step, base + 2)
                nc.gpsimd.tensor_tensor(keep, ones, keep, ALU.mult).then_inc(guard_step, 1)
                pool.wait_ge(guard_step, base + 3)
                settle(pool, fr, pool_settled)
                nc.gpsimd.tensor_scalar(ones, keep, 1.0, None, ALU.add).then_inc(guard_step, 1)
                pool.wait_ge(guard_step, base + 4)
                nc.gpsimd.tensor_tensor(keep, ones, inverse[:, c % 2, :], ALU.mult).then_inc(guard_step, 1)
                pool.wait_ge(guard_step, base + 5)
                wait(pool, inverse_filled, fr.count(CHUNKS, CHUNKS * off + c))
                settle(pool, fr, pool_settled)
                nc.gpsimd.tensor_copy(inverse_wide[:],
                                      keep.rearrange("p (h q) -> p q h", q=2).unsqueeze(3)
                                      .broadcast_to([P, 2, GROUP, HEAD])).then_inc(wide_ready, 1)

            def add_bias(fr, t, off):
                if t == 0:
                    pool.wait_ge(wo_loaded, fr.count(32, 32 * (off + 1)))
                pool.wait_ge(*loaded(fr, t, off))
                nc.gpsimd.tensor_tensor(tile_of(fr, t)[:, t % 2, :], tile_of(fr, t)[:, t % 2, :], bias_o[:], ALU.add).then_inc(res_ready, 1)

            def deviation(fr, t, off):
                done = fr.count(TILES, TILES * off + t + 1)
                pool.wait_ge(stats_ready, done)
                settle(pool, fr, pool_settled)
                nc.gpsimd.tensor_scalar(mean_var[:, t % 2, 1:2], mean_var[:, t % 2, 1:2], EPS, None, ALU.add)\
                    .then_inc(eps_added, 1)
                pool.wait_ge(eps_added, done)
                nc.gpsimd.tensor_tensor(mean_var[:, t % 2, 1:2], mean_var[:, t % 2, 1:2], minus_half, ALU.pow)\
                    .then_inc(deviation_ready, 1)

            def store(fr, t, off):
                pool.wait_ge(normed, fr.count(TILES, TILES * off + t + 1))
                rows = out.rearrange("s (t p) c -> p s t c", p=P)[:, bass.ds(fr.count(1, off), 1), t, :]
                stored = tail_stored[t % 2] if tile_of(fr, t) is x_in else out_stored[t % 2]
                pool.dma_start(rows, tile_of(fr, t)[:, t % 2:t % 2 + 1, :]).then_inc(stored, 16)

            def frame(fr):
                for n in range(fr.slots):
                    for kind, index, off in fr.turns_at(n, 1):
                        if kind == "P" and fr.f != -1:
                            split_lo(pool, fr, index, off)
                        if kind == "P" and fr.f == -1:
                            if index == HEAD_STACK:
                                stack_dmas(pool, pool_settled, [stacked_in_head] * 4, fr, index, off)
                                pool.wait_ge(stacked_in_head, 16 * 4 * GROUP)
                                pool.sem_inc(stacked[HEAD_STACK], 16 * 4 * GROUP)
                    item, off = before(n, CHUNK + 1)
                    if n % CHUNK == 1 and fr.has(off) and (fr.cur or off == -1):
                        widen(fr, item // CHUNK, off)
                    for t in range(TILES):
                        last = TIMETABLE["O", t][-1][0]
                        for at, program in ((last + 2, deviation), (last + 3, store), (SLOT_BIAS[t], add_bias)):
                            if at % ITEMS == n and fr.has(-(at // ITEMS)):
                                program(fr, t, -(at // ITEMS))

            nc.gpsimd.memset(minus_half, -0.5).then_inc(half_set, 1)
            pool.wait_ge(half_set, 1)
            run_frames(pool, frame)
            for s in out_stored:
                pool.wait_ge(s, 16 * (STEPS * TILES // 2 - 1))
            for s in tail_stored:
                pool.wait_ge(s, 16)


def kernel(x, adj, L0_gnn_Wq, L0_gnn_Wk, L0_gnn_Wv, L0_gnn_bv, L0_gnn_Wo, L0_gnn_bo,
           L1_gnn_Wq, L1_gnn_Wk, L1_gnn_Wv, L1_gnn_bv, L1_gnn_Wo, L1_gnn_bo):
    import numpy as np
    import concourse.bacc as bacc
    from concourse.bass_utils import run_bass_kernel_spmd

    weights = np.stack([np.stack([np.asarray(w).T for w in layer]) for layer in
                        ((L0_gnn_Wq, L0_gnn_Wk, L0_gnn_Wv, L0_gnn_Wo), (L1_gnn_Wq, L1_gnn_Wk, L1_gnn_Wv, L1_gnn_Wo))])
    biases = np.stack([np.stack([np.asarray(b) for b in layer]) for layer in
                       ((L0_gnn_bv, L0_gnn_bo), (L1_gnn_bv, L1_gnn_bo))])
    layer_consts = np.array([[[-f, SCALE / f]] * P for f in (2.0, 1.0)], np.float32)
    arrays = {"x": np.asarray(x), "adj": np.asarray(adj), "weights": np.ascontiguousarray(weights),
              "biases": np.ascontiguousarray(biases), "layer_consts": layer_consts,
              "identity": np.eye(P, dtype=np.float32)}
    nc = bacc.Bacc("TRN2", target_bir_lowering=False, num_devices=1)
    args = [nc.dram_tensor(f"in_{n}", a.shape, mybir.dt.from_np(a.dtype), kind="ExternalInput").ap()
            for n, a in arrays.items()]
    out = nc.dram_tensor("out", (STEPS, TOKENS, HIDDEN), F32, kind="ExternalOutput").ap()
    build(nc, *args, out)
    r = run_bass_kernel_spmd(nc, [{f"in_{n}": a for n, a in arrays.items()}], core_ids=[0])
    return r.results[0]["out"][BATCH:]
```
